# Optimizing a Trainium2 kernel written in Bass

```python
import numpy as np
import jax
import jax.numpy as jnp

def _softmax(x, axis=-1):
    return jax.nn.softmax(x, axis=axis)

def _gelu(x):
    return jax.nn.gelu(x, approximate=True)

def _silu(x):
    return jax.nn.silu(x)

def _sigmoid(x):
    return jax.nn.sigmoid(x)

def _layernorm(x, axis=-1, eps=1e-05):
    m = jnp.mean(x, axis=axis, keepdims=True)
    v = jnp.var(x, axis=axis, keepdims=True)
    return (x - m) / jnp.sqrt(v + eps)

def _scatter_add(tgt, idx, src, axis=0):
    return tgt.at[idx].add(src)

def _segment_sum(src, seg, n):
    return jax.ops.segment_sum(src, seg, n)
kernel_name = 'mk_cond_resid_d1_seqx_r2_9e0c90'

def setup_inputs(seed: int=0):
    np.random.seed(seed)
    _w = jnp.asarray

    def _rec_inputs():
        import jax
        import jax.numpy as jnp
        _rk = jax.random.key(seed)
        x = -0.0003929 + 0.9999 * jax.random.normal(jax.random.fold_in(_rk, 1), (2, 2048, 512), jnp.float32)
        _lenS = 2048 - jax.random.randint(jax.random.fold_in(_rk, 7), (2,), 0, max(1, 2048 // 4) + 1, jnp.int32)
        _lenS2 = 2048 - jax.random.randint(jax.random.fold_in(_rk, 8), (2,), 0, max(1, 2048 // 4) + 1, jnp.int32)
        cond_2048 = 0.00782532 + 1.00527 * jax.random.normal(jax.random.fold_in(_rk, 11), (2, 1024), jnp.float32)
        return (x, cond_2048)
    x, cond_2048 = _rec_inputs()

    def _L0_cond_setup():
        import jax, jax.numpy as jnp
        import numpy as np
        B, S, D_MODEL, D_INNER, D_STATE = (4, 2048, 512, 1024, 16)
        key = jax.random.key(seed)
        ks = jax.random.split(key, 12)
        inp = {'x': jax.random.normal(ks[0], (B, S, D_MODEL), jnp.float32), 't_emb': jax.random.normal(ks[1], (B, D_INNER), jnp.float32), 'W_in': jax.random.normal(ks[2], (2 * D_INNER, D_MODEL), jnp.float32) * 0.02, 'W_conv': jax.random.normal(ks[3], (D_INNER, 1, 4), jnp.float32) * 0.1, 'b_conv': jnp.zeros((D_INNER,), jnp.float32), 'ln_g': jnp.ones((D_INNER,), jnp.float32), 'ln_b': jnp.zeros((D_INNER,), jnp.float32), 'W_xproj': jax.random.normal(ks[4], (3 * D_STATE, D_INNER), jnp.float32) * 0.02, 'W_dt': jax.random.normal(ks[5], (D_STATE, D_STATE), jnp.float32) * 0.01, 'b_dt': jax.random.uniform(ks[6], (D_STATE,), jnp.float32) * 0.1, 'A_log': jax.random.normal(ks[7], (D_STATE,), jnp.float32) * 0.1, 'D': jnp.ones((D_INNER,), jnp.float32) * 0.1, 'W_out': jax.random.normal(ks[8], (D_MODEL, D_INNER), jnp.float32) * 0.02}
        return inp
    _L0_cond_all = _L0_cond_setup()
    _L0_cond_in = {k: v for k, v in _L0_cond_all.items() if k in ('W_in', 'W_conv', 'b_conv', 'ln_g', 'ln_b', 'W_xproj', 'W_dt', 'b_dt', 'A_log', 'D', 'W_out')}
    del _L0_cond_all
    return {'x': x, 'cond_2048': cond_2048, 'L0_cond_W_in': _L0_cond_in['W_in'], 'L0_cond_W_conv': _L0_cond_in['W_conv'], 'L0_cond_b_conv': _L0_cond_in['b_conv'], 'L0_cond_ln_g': _L0_cond_in['ln_g'], 'L0_cond_ln_b': _L0_cond_in['ln_b'], 'L0_cond_W_xproj': _L0_cond_in['W_xproj'], 'L0_cond_W_dt': _L0_cond_in['W_dt'], 'L0_cond_b_dt': _L0_cond_in['b_dt'], 'L0_cond_A_log': _L0_cond_in['A_log'], 'L0_cond_D': _L0_cond_in['D'], 'L0_cond_W_out': _L0_cond_in['W_out']}

def reference(x, cond_2048, L0_cond_W_in, L0_cond_W_conv, L0_cond_b_conv, L0_cond_ln_g, L0_cond_ln_b, L0_cond_W_xproj, L0_cond_W_dt, L0_cond_b_dt, L0_cond_A_log, L0_cond_D, L0_cond_W_out):
    import jax
    import jax.numpy as jnp

    def _L0_cond_ref(x, t_emb, W_in, W_conv, b_conv, ln_g, ln_b, W_xproj, W_dt, b_dt, A_log, D, W_out):
        import jax, jax.numpy as jnp
        import numpy as np
        B, S, D_MODEL, D_INNER, D_STATE = (4, 2048, 512, 1024, 16)
        d_inner = W_conv.shape[0]
        d_state = A_log.shape[0]
        xr, gate = jnp.split(x @ W_in.T, 2, axis=-1)
        xr = xr + t_emb[:, None, :]
        xc = jax.lax.conv_general_dilated(xr.transpose(0, 2, 1), W_conv, (1,), [(3, 0)], feature_group_count=d_inner, dimension_numbers=('NCH', 'OIH', 'NCH')) + b_conv[None, :, None]
        xc = jax.nn.silu(xc).transpose(0, 2, 1)
        mu = xc.mean(-1, keepdims=True)
        var = xc.var(-1, keepdims=True)
        xn = (xc - mu) / jnp.sqrt(var + 1e-05) * ln_g + ln_b
        Bm, Cm, dt = jnp.split(xn @ W_xproj.T, 3, axis=-1)
        dt = jnp.tanh(dt @ W_dt.T + b_dt) * 0.01
        A = -jnp.tanh(A_log)
        Ad = 1.0 + dt * A
        Bd = Bm * jnp.minimum(jnp.linalg.norm(xn, axis=-1, keepdims=True), 1.0)
        h0 = jnp.zeros((xn.shape[0], d_state, d_inner), xn.dtype)

        def step(h, inputs):
            ad, bd, xt, ct = inputs
            h = jnp.clip(h * ad[:, :, None] + bd[:, :, None] * xt[:, None, :], -10.0, 10.0)
            yt = jnp.einsum('bd,bdh->bh', ct, h)
            return (h, yt)
        _, ys = jax.lax.scan(step, h0, (Ad.transpose(1, 0, 2), Bd.transpose(1, 0, 2), xn.transpose(1, 0, 2), Cm.transpose(1, 0, 2)))
        y = ys.transpose(1, 0, 2) + D * xn
        return y * jax.nn.silu(gate) @ W_out.T
    x = x + _L0_cond_ref(x, cond_2048, L0_cond_W_in, L0_cond_W_conv, L0_cond_b_conv, L0_cond_ln_g, L0_cond_ln_b, L0_cond_W_xproj, L0_cond_W_dt, L0_cond_b_dt, L0_cond_A_log, L0_cond_D, L0_cond_W_out)
    return x

_drawn_inputs = setup_inputs


def setup_inputs(seed=0):
    import zlib

    import numpy as np

    out = dict(_drawn_inputs(seed))
    spreads = {'L0_cond_b_conv': (0.0, 0.1),
     'L0_cond_ln_g': (1.0, 0.2),
     'L0_cond_ln_b': (0.0, 0.1),
     'L0_cond_D': (0.10000000149011612, 0.6)}
    factors = {'L0_cond_W_dt': 8.0, 'L0_cond_b_dt': 8.0, 'L0_cond_A_log': 8.0}
    for name, (base, spread) in spreads.items():
        noise = np.random.default_rng([zlib.crc32(name.encode()), seed]).standard_normal(out[name].shape)
        drawn = base * np.exp(spread * noise) if base else spread * noise
        out[name] = jnp.asarray(drawn.astype(out[name].dtype))
    for name, factor in factors.items():
        out[name] = (out[name] * factor).astype(out[name].dtype)
    return out
```

```python
import numpy as np

import concourse.bass as bass
from concourse import mybir
from contextlib import ExitStack

BATCH, SEQ, DM, DI, NS, TAPS = 2, 2048, 512, 1024, 16, 4
P = 128
DB = DI // P
CB = DM // P
STEPS = BATCH * SEQ // P
SUB = 32
NSUB = P // SUB
NQ = 4
QN = NS // NQ
WAYS = P // NS
TILES = DB * NQ
BANK = 512
CLIP = 10.0
EPS = 1e-5
RING = 2
LAG = 4


def row_steps():
    return np.arange(P).reshape(WAYS, NS).T.reshape(-1)


def shape_constants():
    s = np.arange(P)
    t = np.arange(P)
    step = row_steps()
    tri = ((s[:, None] <= step[None, :]) & (s[:, None] >= 1)).astype(np.float32)
    shuffle = (t[:, None] == step[None, :]).astype(np.float32)
    r = np.arange(SUB)
    sub = ((r[:, None] <= r[None, :]) & (r[:, None] >= 1)).astype(np.float32)
    sub = np.tile(sub, (NSUB, 1))
    heads = np.array([SUB * jj for jj in range(NSUB)] + [P - 1])
    prefix = ((s[:, None] <= heads[None, :]) & (s[:, None] >= 1)).astype(np.float32)
    delta = np.tile(np.eye(WAYS, dtype=np.float32), (NS, 1))
    low = np.where((s % SUB) >= NS, -1.0, 0.0).astype(np.float32)[:, None]
    c128 = np.concatenate([np.eye(P, dtype=np.float32), tri, shuffle, sub, prefix, delta, low], axis=1)
    twice = np.tile(np.eye(NS, dtype=np.float32), (1, P // NS))
    spread = np.repeat(np.eye(NS, dtype=np.float32), WAYS, axis=1)
    c16 = np.concatenate([twice, spread], axis=1)
    carry = np.zeros((2, NS, NSUB, 2, NS, SUB), np.float16)
    for n in range(NS):
        carry[:, n, :, :, n, :] = -1.0
    carry[:, :, 0, :, :, 0] = 0.0
    ones = np.ones((1, NSUB * DI), np.float16)
    return {"c128": c128, "c16": c16, "carry": carry.reshape(2 * NS, -1), "ones16": ones}


SEMS = """
xT_in gate_x_in res_in out_done0 out_done1 const_in
xstack_in0 xstack_in1 stack_in0 stack_in1 bound_out bound_in0 bound_in1
rows_ready ones_ready gw_ready sums_ready sums_taken halo_set prep rowbc_ready rowbc_taken p16 act_prep
lower_ready upper_ready upper_copied scanned flipped flip_copied
xr_ready xr_taken xt_ready xt_taken z_ready z_taken zT_ready zT_taken dt_ready dt_taken
mb_ready mb_taken cr_ready cr_taken hin_ready hin_taken carry_ready carry_taken
hend_ready hend_taken y_ready y_taken yT_ready yT_taken gate_ready gate_taken
out_ready out_taken
conv_done tap tap_made silu_done stats aggr rstd moments z1 zb ad scan_p recip weighted bound16 bound_all
norm_in xa xg xn_done xh_done xl_done squares root nrm nb16 tt_done dx_done kend_done y_gated h1_done
carry16
""".split()


def build(nc, A, out, scratch):
    F, H = mybir.dt.float32, mybir.dt.float16
    ALU, ACT = mybir.AluOpType, mybir.ActivationFunctionType
    with ExitStack() as S:
        def sb(name, shape, dt=F):
            return S.enter_context(nc.sbuf_tensor(name, shape, dt))

        sem = {n: S.enter_context(nc.semaphore(n)) for n in SEMS}

        w_in = sb("w_in", [P, CB, 2 * DI])
        w_out = sb("w_out", [P, DB, DM])
        c128 = sb("c128_sb", [P, 3 * P + SUB + NSUB + 1 + WAYS + 1])
        at = 0
        parts = []
        for width in (P, P, P, SUB, NSUB + 1, WAYS, 1):
            parts.append(c128[:, at:at + width])
            at += width
        ident, tri, shuffle, submask, prefix, delta, neg_low = parts
        c16 = sb("c16_sb", [NS, 2 * P])
        twice = c16[:, 0:P]
        spread = c16[:, P:2 * P]
        cols = sb("cols_sb", [P, DB, 3 + TAPS + BATCH])
        small = sb("small_sb", [NS, 3 * NS + 2])
        row_g = sb("row_g", [P, DI])
        row_b = sb("row_b", [P, DI])
        row_d = sb("row_d", [P, DI])
        gw = sb("gw", [P, DB, 3 * NS])
        sums = sb("sums", [P, 2, 3 * NS])
        conv_b = sb("conv_b", [P, BATCH, DB])
        a01 = sb("a01", [NS, 2])
        halfs = sb("halfs", [P, 2])
        idle = sb("idle", [P, 2, 16])
        zeros = sb("zeros", [NS, P])

        xT = sb("xT", [P, CB, P])
        xTg = sb("xTg", [P, CB, P])
        xr = sb("xr", [P, BATCH, DB, TAPS - 1 + P])
        conv = sb("conv", [P, DB, P])
        xcT = sb("xcT", [P, DB, P])
        yT = xcT
        xc = sb("xc", [P, DI])
        tapped = xc[:].rearrange("d (c t) -> d c t", c=DB)
        wx = conv[:, :, 0:3 * NS]
        bw = conv[:, :, 3 * NS:6 * NS] if 6 * NS <= P else tapped[:, :, 0:3 * NS]
        ws = sb("ws", [P, 5, DB])
        xn = sb("xn", [P, 2, DI])
        xh = sb("xh", [P, DI], H)
        xl = sb("xl", [P, DI], H)
        st = sb("st", [P, 2, 6])
        mom = sb("mom", [P, 2])
        tiny = sb("tiny", [P, 8])

        z = sb("z", [P, 3 * NS])
        z1 = sb("z1", [P, 3 * NS])
        z2 = sb("z2", [P, 3 * NS])
        zT = sb("zT", [NS, 3, P])
        th = sb("th", [NS, P])
        ad = sb("ad", [NS, P])
        a0 = sb("a0", [NS, 2])
        pf = sb("pf", [NS, 2, P])
        p_end = sb("p_end", [NS, 2])
        bc = sb("bc", [NS, 2, 2, P])
        bnd = sb("bnd", [NS, 2, P])
        bnd16 = sb("bnd16", [NS, 2, 2, P], H)
        mT = sb("mT", [P, 2, P])
        nbh = sb("nbh", [P, NS], H)
        nbl = sb("nbl", [P, NS], H)
        bq = sb("bq", [P, NS])
        bqm = sb("bqm", [P, 2, NSUB + 1, 2, NS])
        cst = sb("cst", [P, 4, 4, SUB])
        tth = sb("tth", [P, NS, SUB], H)
        ttl = sb("ttl", [P, NS, SUB], H)
        h1 = sb("h1", [NS, 2, DI])
        ch = xh
        cc = xl

        xs = sb("xs", [P, 2, NSUB, DI], H)
        ts = sb("ts", [P, 2, NSUB, 2, NS * SUB], H)

        upper = sb("upper", [P, RING, BANK])
        ks = sb("ks", [P, 2, NS, P])
        kend = sb("kend", [P, 2, DB, NS])
        kT = sb("kT", [P, 2, 4, 4, P])

        gate = sb("gate", [P, DI])
        y = sb("y", [P, DI])
        ones = y[:, 0:P]
        dx = sb("dx", [P, DI])
        res = sb("res", [P, DM])

        ps_low = S.enter_context(nc.psum_tensor("ps_low", [P, 2, BANK], F))
        ps_up = S.enter_context(nc.psum_tensor("ps_up", [P, 2, BANK], F))
        ps_flip = S.enter_context(nc.psum_tensor("ps_flip", [P, 2, BANK], F))
        ps_job = S.enter_context(nc.psum_tensor("ps_job", [P, 2, BANK], F))

        def since(eng, name, value):
            if isinstance(value, int) and value <= 0:
                return
            eng.wait_ge(sem[name], value)

        JOBS = [(0, "z", 0, 1, 1), (1, "y", 6, -1, 8), (1, "yT", 0, -1, 2), (5, "y", 7, -1, 8),
                (6, "hend", 0, -1, 2), (6, "cr", 0, 0, 1), (7, "hend", 1, -1, 2), (7, "xr", 0, 2, 2),
                (8, "xr", 1, 2, 2), (9, "y", 0, 0, 8), (10, "yT", 1, -1, 2), (10, "gate", 0, 0, 2),
                (11, "out", 0, -1, 1), (13, "y", 1, 0, 8), (13, "zT", 0, 1, 1), (14, "gate", 1, 0, 2),
                (15, "dt", 0, 1, 1), (17, "y", 2, 0, 8), (18, "xt", 0, 2, 2), (19, "mb", 0, 1, 1),
                (21, "y", 3, 0, 8), (21, "hin", 0, 1, 2), (22, "hin", 1, 1, 2), (23, "xt", 1, 2, 2),
                (25, "y", 4, 0, 8), (25, "carry", 0, 1, 2), (26, "carry", 1, 1, 2), (29, "y", 5, 0, 8)]
        assert len(JOBS) % 2 == 0
        BANK_OF = {(name, i): m % 2 for m, (_, name, i, _, _) in enumerate(JOBS)}

        def exists(k, off):
            return not isinstance(k, int) or 0 <= k + off < STEPS

        def bank_free(pe, k, m):
            kk, mm = k, m
            while True:
                mm -= 2
                if mm < 0:
                    mm += len(JOBS)
                    kk = kk - 1
                    if isinstance(kk, int) and kk < -2:
                        return
                _, name, i, off, per = JOBS[mm]
                if exists(kk, off):
                    pe.wait_ge(sem[name + "_taken"], (kk + off) * per + i + 1)
                    return

        def steps(eng, body):
            for k in range(-2, 2):
                body(k, k % 2)
            with eng.Fori(2, STEPS - 2, 2) as k0:
                body(k0, 0)
                body(k0 + 1, 1)
            for k in range(STEPS - 2, STEPS + 1):
                body(k, k % 2)

        block = S.enter_context(nc.Block())

        @block.sync
        def _(sp):
            loads = [(w_in[:], A["w_inT"].rearrange("(c p) d -> p c d", p=P)),
                     (w_out[:], A["w_outT"].rearrange("(c p) d -> p c d", p=P)),
                     (c128[:], A["c128"]), (c16[:], A["c16"]),
                     (cols[:], A["cols"]), (wx, A["wxT"].rearrange("(c p) m -> p c m", p=P)),
                     (small[:], A["small"]),
                     (row_g[0:1], A["rows"][0:1]), (row_b[0:1], A["rows"][1:2]), (row_d[0:1], A["rows"][2:3])]
            for p in range(2):
                carry = A["carry"].rearrange("r (j c) -> r j c", j=NSUB)
                loads.append((ts[96:128, p].rearrange("r j v c -> r j (v c)"), carry))
                for r in (0, 32):
                    loads.append((xs[r:r + 1, p], A["ones16"].rearrange("o (j d) -> o j d", j=NSUB)))
            for dst, src in loads:
                sp.dma_start(dst, src).then_inc(sem["const_in"], 16)

            xT_dram = A["xT"].rearrange("b (c p) t -> b p c t", p=P)
            xTs_dram = A["xTs"].rearrange("b (c p) t -> b p c t", p=P)
            x_dram = A["x"]

            def body(k, p):
                def chunk(off):
                    b = (p + off) % 2
                    c = (k + off - b) // 2 if isinstance(k, int) else (k + (off - b)) // 2
                    return b, c

                if exists(k, 2):
                    b, c = chunk(2)
                    since(sp, "xr_ready", 2 * (k + 2))
                    sp.dma_start(xT[:], xT_dram[b, :, :, bass.ds(c * P, P)]).then_inc(sem["xT_in"], 16)
                if exists(k, 0):
                    b, c = chunk(0)
                    since(sp, "gate_ready", 2 * k)
                    sp.dma_start(xTg[:], xTs_dram[b, :, :, bass.ds(c * P, P)]).then_inc(sem["gate_x_in"], 16)
                if exists(k, -1):
                    b, c = chunk(-1)
                    if not (isinstance(k, int) and k < 2):
                        sp.wait_ge(sem[f"out_done{p}"], 16 * ((k - p) // 2))
                    sp.dma_start(res[:], x_dram[b, bass.ds(c * P, P), :]).then_inc(sem["res_in"], 16)
                    sp.wait_ge(sem["out_taken"], k)
                    sp.dma_start(out[b, bass.ds(c * P, P), :], res[:]).then_inc(sem[f"out_done{b}"], 16)
                if exists(k, 1):
                    j, pn = k + 1, (p + 1) % 2
                    xstack, stack = sem[f"xstack_in{pn}"], sem[f"stack_in{pn}"]
                    sp.wait_ge(sem["bound_all"], j + 1)
                    for h in range(2):
                        sp.dma_start(scratch[h], bnd16[:, h]).then_inc(sem["bound_out"], 16)
                    since(sp, "upper_ready", TILES * k)
                    sp.wait_ge(sem["xh_done"], j + 1)
                    sp.wait_ge(sem["xl_done"], j + 1)
                    for jj in range(NSUB):
                        a = SUB * jj
                        sp.dma_start(xs[1:SUB, pn, jj], xh[a + 1:a + SUB]).then_inc(xstack, 16)
                        sp.dma_start(xs[SUB + 1:2 * SUB, pn, jj], xh[a + 1:a + SUB]).then_inc(xstack, 16)
                        sp.dma_start(xs[2 * SUB:3 * SUB, pn, jj], xl[a:a + SUB]).then_inc(xstack, 16)
                    sp.wait_ge(sem["bound_out"], 32 * (j + 1))
                    for h in range(2):
                        for v in range(2):
                            src = scratch[h].rearrange("(o n) v (j t) -> o v j n t", o=1, j=NSUB)[:, v]
                            dst = ts[SUB * h:SUB * h + 1, pn, :, v].rearrange("o j (n t) -> o j n t", n=NS)
                            for jj in range(NSUB):
                                sp.dma_start(dst[:, jj], src[:, jj]).then_inc(sem[f"bound_in{pn}"], 16)
                    sp.wait_ge(sem["tt_done"], 2 * (j + 1))
                    for jj in range(NSUB):
                        a = SUB * jj
                        for v in range(2):
                            hi, lo = (t[:].rearrange("s n t -> s (n t)") for t in (tth, ttl))
                            sp.dma_start(ts[1:SUB, pn, jj, v], hi[a + 1:a + SUB]).then_inc(stack, 16)
                            sp.dma_start(ts[SUB + 1:2 * SUB, pn, jj, v], lo[a + 1:a + SUB]).then_inc(stack, 16)
                            sp.dma_start(ts[2 * SUB:3 * SUB, pn, jj, v], hi[a:a + SUB]).then_inc(stack, 16)
                    for h in range(2):
                        sp.wait_ge(sem["carry_taken"], 2 * j + h + 1)
                        for jj in range(NSUB):
                            cut = slice(h * BANK, (h + 1) * BANK)
                            sp.dma_start(xs[3 * SUB:P, pn, jj, cut],
                                         cc[SUB * jj:SUB * jj + SUB, cut]).then_inc(stack, 16)

            steps(sp, body)
            for b in range(BATCH):
                sp.wait_ge(sem[f"out_done{b}"], 16 * (STEPS // BATCH))
            sp.wait_ge(sem["bound_out"], 32 * STEPS)

        N_CONST = 16 * 16
        N_XSTACK = 16 * 3 * NSUB
        N_STACK = 16 * (6 * NSUB + 2 * NSUB)
        N_BOUND = 16 * 4 * NSUB

        def pair(k, p, off):
            q = (p + off) % 2
            return (k + off - q) // 2 + 1

        @block.tensor
        def _(pe):
            mm = nc.tensor.matmul
            tr = nc.tensor.transpose
            pe.wait_ge(sem["const_in"], N_CONST)
            pe.wait_ge(sem["prep"], 1)
            for i, row in enumerate((row_g, row_b, row_d)):
                for h in range(2):
                    n = 2 * i + h
                    if n >= 2:
                        pe.wait_ge(sem["rowbc_taken"], n - 1)
                    mm(ps_job[:, n % 2], ones[0:1, :], row[0:1, h * BANK:(h + 1) * BANK],
                       start=True, stop=True).then_inc(sem["rowbc_ready"], 1)
            pe.wait_ge(sem["gw_ready"], 2)
            for i, src in enumerate((gw, bw)):
                for c in range(DB):
                    last = mm(ps_up[:, i, 0:3 * NS], ones, src[:, c], start=(c == 0), stop=(c == DB - 1))
                last.then_inc(sem["sums_ready"], 1)
            pe.wait_ge(sem["sums_taken"], 1)
            pe.wait_ge(sem["rowbc_taken"], 6)

            def job(k, p, m):
                _, name, i, off, per = JOBS[m]
                if not exists(k, off):
                    return
                j = k + off
                q = (p + off) % 2
                ps = ps_job[:, m % 2]
                ready = sem[name + "_ready"]
                half = slice(i * BANK, (i + 1) * BANK)
                if name == "xr":
                    pe.wait_ge(sem["xT_in"], 16 * (j + 1))
                elif name == "gate":
                    pe.wait_ge(sem["gate_x_in"], 16 * (j + 1))
                elif name == "xt":
                    pe.wait_ge(sem["silu_done"], j + 1)
                elif name == "z":
                    pe.wait_ge(sem["silu_done"], j + 1)
                elif name == "zT":
                    pe.wait_ge(sem["zb"], j + 1)
                elif name == "dt":
                    pe.wait_ge(sem["zT_taken"], j + 1)
                elif name == "mb":
                    pe.wait_ge(sem["weighted"], j + 1)
                elif name == "cr":
                    pe.wait_ge(sem["weighted"], j + 1)
                elif name == "hin":
                    pe.wait_ge(sem["zb"], j + 1)
                    pe.wait_ge(sem["xn_done"], j + 1)
                elif name == "carry":
                    pe.wait_ge(sem["mb_taken"], j + 1)
                    pe.wait_ge(sem["h1_done"], 2 * j + i + 1)
                elif name == "hend":
                    pe.wait_ge(sem["kend_done"], DB * (j + 1))
                elif name == "y":
                    pe.wait_ge(sem["flip_copied"], TILES * j + NQ * (i + 1))
                    if i == 0:
                        pe.wait_ge(sem["cr_taken"], j + 1)
                    if i % 4 == 0:
                        pe.wait_ge(sem["dx_done"], 2 * j + i // 4 + 1)
                elif name == "yT":
                    pe.wait_ge(sem["y_gated"], 2 * j + i + 1)
                elif name == "out":
                    pe.wait_ge(sem["yT_taken"], 2 * (j + 1))
                bank_free(pe, k, m)
                if name == "xr":
                    for e in range(4):
                        for c in range(CB):
                            last = mm(ps[:, e * P:(e + 1) * P], w_in[:, c, (4 * i + e) * P:(4 * i + e + 1) * P],
                                      xT[:, c, :], start=(c == 0), stop=(c == CB - 1))
                elif name == "gate":
                    for c in range(CB):
                        last = mm(ps, xTg[:, c, :], w_in[:, c, DI + i * BANK:DI + (i + 1) * BANK],
                                  start=(c == 0), stop=(c == CB - 1))
                elif name == "xt":
                    for e in range(4):
                        last = tr(ps[:, e * P:(e + 1) * P], xcT[:, 4 * i + e, :], ident)
                elif name == "z":
                    for c in range(DB):
                        last = mm(ps[:, 0:3 * NS], xcT[:, c, :], gw[:, c, :], start=(c == 0), stop=(c == DB - 1))
                elif name == "zT":
                    for e in range(3):
                        last = tr(ps[0:NS, e * P:(e + 1) * P], z[:, e * NS:(e + 1) * NS], ident)
                elif name == "dt":
                    last = mm(ps[0:3 * NS, 0:P], small[:, 0:3 * NS], zT[:, 2, :], start=True, stop=True)
                elif name == "mb":
                    mm(ps[:, 0:P], bc[:, q, 0, :], bc[:, q, 1, :], start=True, stop=True)
                    last = tr(ps[:, P:P + NS], bc[:, q, 0, :], ident[0:NS, 0:NS])
                elif name == "cr":
                    last = mm(ps[:, 0:P], spread, bc[:, q, 1, :], start=True, stop=True)
                elif name == "hin":
                    last = mm(ps[0:3 * NS], z[0:1, :], xn[0:1, q, half], start=True, stop=True)
                elif name == "carry":
                    mm(ps, twice, h1[:, q, half], start=True, stop=False)
                    last = mm(ps, bqm[:, q, 0:NSUB].rearrange("s j d n -> s (j d n)"), xn[:, q, half],
                              start=False, stop=True)
                elif name == "hend":
                    mm(ps[0:NS], bqm[:, q, NSUB, 0, :], xn[:, q, half], start=True, stop=False)
                    mm(ps[0:NS], ident[0:NS, 0:NS], h1[:, q, half], start=False, stop=False)
                    for e in range(4):
                        last = mm(ps[0:NS, e * P:(e + 1) * P], kend[:, q, 4 * i + e, :], ident,
                                  start=False, stop=(e == 3))
                elif name == "y":
                    mm(ps[:, 0:P], mT[:, q, :], xn[:, q, i * P:(i + 1) * P], start=True, stop=False)
                    mm(ps[:, 0:P], bc[:, q, 1, :], h1[:, q, i * P:(i + 1) * P], start=False, stop=False)
                    mm(ps[:, 0:P], shuffle, dx[:, i * P:(i + 1) * P], start=False, stop=False)
                    for e in range(4):
                        for g in range(4):
                            last = mm(ps[SUB * g:SUB * (g + 1), 0:P], cst[:, g, e, :], kT[:, i % 2, g, e, :],
                                      start=False, stop=(e == 3))
                elif name == "yT":
                    for e in range(4):
                        d = 4 * i + e
                        last = tr(ps[:, e * P:(e + 1) * P], y[:, d * P:(d + 1) * P], ident)
                elif name == "out":
                    for c in range(DB):
                        last = mm(ps, yT[:, c, :], w_out[:, c, :], start=(c == 0), stop=(c == DB - 1))
                last.then_inc(ready, 1)

            def fill(k, p, s):
                g = TILES * k + s
                u, q = divmod(s, NQ)
                if s == 0:
                    pe.wait_ge(sem[f"xstack_in{p}"], N_XSTACK * pair(k, p, 0))
                    pe.wait_ge(sem[f"stack_in{p}"], N_STACK * pair(k, p, 0))
                    pe.wait_ge(sem[f"bound_in{p}"], N_BOUND * pair(k, p, 0))
                for v, ps, free, ready in ((1, ps_up, "upper_copied", "upper_ready"),
                                           (0, ps_low, "scanned", "lower_ready")):
                    since(pe, free, g - 1)
                    o = ps[:, s % 2].rearrange("d (n t) -> d n t", n=QN)
                    for jj in range(NSUB):
                        last = mm(o[:, :, SUB * jj:SUB * (jj + 1)], xs[:, p, jj, u * P:(u + 1) * P],
                                  ts[:, p, jj, v, q * QN * SUB:(q + 1) * QN * SUB].rearrange("s (n t) -> s n t", n=QN),
                                  start=True, stop=True)
                    last.then_inc(sem[ready], 1)

            def flip(k, p, s):
                g = TILES * k + s
                u, q = divmod(s, NQ)
                if q == 0:
                    pe.wait_ge(sem["scanned"], g + NQ)
                since(pe, "flip_copied", g - 1)
                flat = ks[:, u % 2].rearrange("d n t -> d (n t)")
                for e in range(4):
                    last = tr(ps_flip[:, s % 2, e * P:(e + 1) * P], flat[:, bass.ds(4 * q + e, P, step=NS)], ident)
                last.then_inc(sem["flipped"], 1)

            def body(k, p):
                m = 0
                for s in range(TILES):
                    if exists(k, 0) and s == 0:
                        fill(k, p, 0)
                    if exists(k, 0) and s + 1 < TILES:
                        fill(k, p, s + 1)
                    t = s - LAG
                    if t >= 0 and exists(k, 0):
                        flip(k, p, t)
                    elif t < 0 and exists(k, -1):
                        flip(k - 1, 1 - p, t + TILES)
                    while m < len(JOBS) and JOBS[m][0] == s:
                        job(k, p, m)
                        m += 1

            steps(pe, body)

        @block.scalar
        def _(act):
            copy, act_fn = nc.scalar.copy, nc.scalar.activation
            act.wait_ge(sem["const_in"], N_CONST)
            act_fn(tiny[:, 7:8], cols[:, 0, 0:1], ACT.Silu).then_inc(sem["act_prep"], 1)
            act_fn(a01[:, 0:1], small[:, 3 * NS + 1:3 * NS + 2], ACT.Tanh).then_inc(sem["act_prep"], 1)
            for i, row in enumerate((row_g, row_b, row_d)):
                for h in range(2):
                    n = 2 * i + h
                    act.wait_ge(sem["rowbc_ready"], n + 1)
                    if h:
                        act.wait_ge(sem["rowbc_ready"], n + 1)
                    copy(row[:, h * BANK:(h + 1) * BANK], ps_job[:, n % 2]).then_inc(sem["rowbc_taken"], 1)
            act.wait_ge(sem["sums_ready"], 2)
            copy(sums[:], ps_up[:, :, 0:3 * NS]).then_inc(sem["sums_taken"], 1)

            def bank(name, i=0):
                return ps_job[:, BANK_OF[name, i]]

            def side(k, p, s):
                def take(name, i, off, per):
                    act.wait_ge(sem[name + "_ready"], (k + off) * per + i + 1)

                if s in (7, 8) and exists(k, -1):
                    i, q = s - 7, (p + 1) % 2
                    take("hend", i, -1, 2)
                    act_fn(h1[:, q, i * BANK:(i + 1) * BANK], bank("hend", i)[0:NS], ACT.Identity,
                           scale=p_end[:, q:q + 1]).then_inc(sem["hend_taken"], 1)
                if s == 7 and exists(k, 1):
                    j, q = k + 1, (p + 1) % 2
                    act.wait_ge(sem["moments"], j + 1)
                    act.wait_ge(sem["xt_taken"], 2 * (j + 1))
                    since(act, "y_ready", DB * k)
                    since(act, "hend_ready", 2 * k)
                    act_fn(xn[:, q], xc[:], ACT.Identity, scale=tiny[:, 1:2],
                           bias=tiny[:, 3:4]).then_inc(sem["xa"], 1)
                if s in (8, 9) and exists(k, 2):
                    i = s - 8
                    take("xr", i, 2, 2)
                    since(act, "conv_done", k + 1)
                    copy(xr[:, p, 4 * i:4 * i + 4, TAPS - 1:],
                         bank("xr", i).rearrange("d (e t) -> d e t", e=4)).then_inc(sem["xr_taken"], 1)
                if s in (2, 11) and exists(k, -1):
                    i = (s - 2) // 9
                    take("yT", i, -1, 2)
                    for e in range(4):
                        last = copy(yT[:, 4 * i + e, :].rearrange("d (i r) -> d r i", r=NS),
                                    bank("yT", i)[:, e * P:(e + 1) * P].rearrange("d (r i) -> d r i", i=WAYS))
                    last.then_inc(sem["yT_taken"], 1)
                if s == 11 and exists(k, 1):
                    j, q = k + 1, (p + 1) % 2
                    act.wait_ge(sem["xn_done"], j + 1)
                    since(act, "carry_taken", 2 * j)
                    act_fn(ch[:], xn[:, q], ACT.Square, accum_out=tiny[:, 4:5]).then_inc(sem["squares"], 1)
                    act.wait_ge(sem["squares"], j + 1)
                    act_fn(xh[:], xn[:, q], ACT.Identity).then_inc(sem["xh_done"], 1)
                if s in (11, 15) and exists(k, 0):
                    i = (s - 11) // 4
                    take("gate", i, 0, 2)
                    since(act, "y_gated", 2 * (k - 1) + i + 1)
                    act_fn(gate[:, i * BANK:(i + 1) * BANK], bank("gate", i), ACT.Silu).then_inc(sem["gate_taken"], 1)
                if s == 14 and exists(k, 1):
                    take("zT", 0, 1, 1)
                    copy(zT[:], bank("zT")[0:NS, 0:3 * P].rearrange("n (e t) -> n e t", e=3)
                         ).then_inc(sem["zT_taken"], 1)
                if s == 16 and exists(k, 1):
                    take("dt", 0, 1, 1)
                    act_fn(th[:], bank("dt")[0:NS, 0:P], ACT.Tanh, bias=small[:, 3 * NS:3 * NS + 1]
                           ).then_inc(sem["dt_taken"], 1)
                if s == 17 and exists(k, 2):
                    act.wait_ge(sem["tap"], 3 * (k + 3))
                    since(act, "z_ready", min(k + 2, STEPS) if isinstance(k, int) else k + 2)
                    since(act, "out_ready", k)
                    act_fn(xcT[:], conv[:], ACT.Silu).then_inc(sem["silu_done"], 1)
                if s in (19, 24) and exists(k, 2):
                    i = (s - 19) // 5
                    take("xt", i, 2, 2)
                    since(act, "xa", k + 2)
                    copy(xc[:, i * BANK:(i + 1) * BANK], bank("xt", i)).then_inc(sem["xt_taken"], 1)
                if s in (26, 27) and exists(k, 1):
                    i = s - 26
                    take("carry", i, 1, 2)
                    act.wait_ge(sem[f"xstack_in{1 - p}"], N_XSTACK * pair(k, p, 1))
                    copy(ch[:, i * BANK:(i + 1) * BANK], bank("carry", i)).then_inc(sem["carry16"], 1)

            def copy_flip(k, p, s):
                g = TILES * k + s
                u, q = divmod(s, NQ)
                act.wait_ge(sem["flipped"], g + 1)
                since(act, "y_ready", DB * k + u - 1)
                copy(kT[:, u % 2, q], ps_flip[:, s % 2].rearrange("r (e d) -> r e d", e=4)
                     ).then_inc(sem["flip_copied"], 1)

            def body(k, p):
                for s in range(TILES):
                    if exists(k, 0):
                        g = TILES * k + s
                        act.wait_ge(sem["upper_ready"], g + 1)
                        since(act, "scanned", g - RING + 1)
                        copy(upper[:, s % RING], ps_up[:, s % 2]).then_inc(sem["upper_copied"], 1)
                    t = s - LAG
                    if t >= 0 and exists(k, 0):
                        copy_flip(k, p, t)
                    elif t < 0 and exists(k, -1):
                        copy_flip(k - 1, 1 - p, t + TILES)
                    side(k, p, s)

            steps(act, body)

        @block.vector
        def _(dve):
            tt, tsc, stt = nc.vector.tensor_tensor, nc.vector.tensor_scalar, nc.vector.scalar_tensor_tensor
            nc.vector.memset(ones, 1.0)
            nc.vector.memset(zeros[:], 0.0)
            nc.vector.memset(halfs[:, 0:1], -0.5)
            nc.vector.memset(halfs[:, 1:2], 0.5)
            nc.vector.memset(pf[:, 1, 0:1], 1.0)
            nc.vector.memset(cst[:], 0.0)
            nc.vector.memset(bqm[:], 0.0).then_inc(sem["prep"], 1)
            dve.wait_ge(sem["const_in"], N_CONST)
            tt(gw[:], wx, cols[:, :, 0:1].broadcast_to([P, DB, 3 * NS]), ALU.mult).then_inc(sem["gw_ready"], 1)
            tt(bw, wx, cols[:, :, 1:2].broadcast_to([P, DB, 3 * NS]), ALU.mult).then_inc(sem["gw_ready"], 1)
            tap0 = 3
            tt(ws[:, 0, :], cols[:, :, tap0], cols[:, :, tap0 + 1], ALU.add).then_inc(sem["p16"], 1)
            tt(ws[:, 1, :], cols[:, :, tap0 + 2], cols[:, :, tap0 + 3], ALU.add).then_inc(sem["p16"], 1)
            dve.wait_ge(sem["p16"], 2)
            tt(ws[:, 2, :], ws[:, 0, :], ws[:, 1, :], ALU.add).then_inc(sem["p16"], 1)
            dve.wait_ge(sem["p16"], 3)
            for b in range(BATCH):
                cond = cols[:, :, 3 + TAPS + b]
                tt(ws[:, 3 + b, :], ws[:, 2, :], cond, ALU.mult).then_inc(sem["p16"], 1)
                dve.wait_ge(sem["p16"], 4 + b)
                tt(conv_b[:, b, :], ws[:, 3 + b, :], cols[:, :, 2], ALU.add)
                tsc(xr[:, b, :, 0:TAPS - 1],
                    cols[:, :, 3 + TAPS + b:4 + TAPS + b].broadcast_to([P, DB, TAPS - 1]),
                    -1.0, None, ALU.mult).then_inc(sem["halo_set"], 1)
            dve.wait_ge(sem["act_prep"], 2)
            tsc(a01[:, 1:2], a01[:, 0:1], -0.01, None, ALU.mult).then_inc(sem["p16"], 1)
            dve.wait_ge(sem["p16"], 6)

            def bank(name, i=0):
                return ps_job[:, BANK_OF[name, i]]

            def side(k, p, s):
                j, q = k + 1, (p + 1) % 2
                if s == 0 and exists(k, 1):
                    dve.wait_ge(sem["xt_taken"], 2 * (j + 1))
                    nc.vector.bn_stats(st[:, 0], xc[:, 0:BANK]).then_inc(sem["stats"], 1)
                    nc.vector.bn_stats(st[:, 1], xc[:, BANK:]).then_inc(sem["stats"], 1)
                    dve.wait_ge(sem["stats"], 2 * (j + 1))
                    since(dve, "xa", j)
                    nc.vector.memset(tiny[:, 7:8], 0.0)
                    nc.vector.bn_aggr(mom[:], st[:].rearrange("p a b -> p (a b)")).then_inc(sem["aggr"], 1)
                    dve.wait_ge(sem["aggr"], j + 1)
                    tsc(tiny[:, 0:1], mom[:, 1:2], EPS, None, ALU.add)
                    tsc(tiny[:, 2:3], mom[:, 0:1], -1.0, None, ALU.mult).then_inc(sem["norm_in"], 1)
                if s == 1 and exists(k, 1):
                    dve.wait_ge(sem["norm_in"], j + 1)
                    dve.wait_ge(sem["z_ready"], j + 1)
                    stt(z1[:], sums[:, 0, :], tiny[:, 2:3], bank("z")[:, 0:3 * NS], ALU.mult, ALU.add
                        ).then_inc(sem["z_taken"], 1)
                if s == 3 and exists(k, 1):
                    dve.wait_ge(sem["rstd"], j + 1)
                    tsc(tiny[:, 3:4], tiny[:, 2:3], tiny[:, 1:2], None, ALU.mult).then_inc(sem["moments"], 1)
                    dve.wait_ge(sem["z_taken"], j + 1)
                    stt(z2[:], z1[:], tiny[:, 1:2], sums[:, 1, :], ALU.mult, ALU.add).then_inc(sem["z1"], 1)
                if s == 12 and exists(k, 1):
                    dve.wait_ge(sem["nrm"], j + 1)
                    dve.wait_ge(sem["z1"], j + 1)
                    since(dve, "zT_ready", j)
                    since(dve, "hin_ready", 2 * j)
                    nc.vector.tensor_copy(z[:, NS:3 * NS], z2[:, NS:3 * NS])
                    tsc(z[:, 0:NS], z2[:, 0:NS], tiny[:, 6:7], None, ALU.mult).then_inc(sem["zb"], 1)
                if s == 17 and exists(k, 1):
                    dve.wait_ge(sem["dt_taken"], j + 1)
                    since(dve, "weighted", j)
                    tsc(ad[:], th[:], a01[:, 1:2], 1.0, ALU.mult, ALU.add).then_inc(sem["ad"], 1)
                    dve.wait_ge(sem["ad"], j + 1)
                    nc.vector.tensor_tensor_scan(pf[:, 1, 1:], ad[:, 1:], zeros[:, 1:], 1.0,
                                                 ALU.mult, ALU.add).then_inc(sem["scan_p"], 1)
                    dve.wait_ge(sem["scan_p"], j + 1)
                    nc.vector.reciprocal(pf[:, 0], pf[:, 1]).then_inc(sem["recip"], 1)
                    since(dve, "hend_taken", 2 * k)
                    nc.vector.tensor_copy(p_end[:, q:q + 1], pf[:, 1, P - 1:P])
                    nc.vector.tensor_copy(a0[:, q:q + 1], ad[:, 0:1])
                    dve.wait_ge(sem["recip"], j + 1)
                    since(dve, "y_ready", DB * k)
                    tt(bc[:, q, 0], zT[:, 0], pf[:, 0], ALU.mult)
                    tt(bc[:, q, 1].rearrange("n (r i) -> n i r", i=WAYS), zT[:, 1].rearrange("n (i r) -> n i r", r=NS),
                       pf[:, 1].rearrange("n (i r) -> n i r", r=NS), ALU.mult).then_inc(sem["weighted"], 1)
                    since(dve, "bound_out", 32 * j)
                    nc.vector.memset(bnd[:, :, 0:1], 0.0)
                    tsc(bnd[:, 0, 1:], pf[:, 0, 1:], -CLIP, None, ALU.mult)
                    tsc(bnd[:, 1, 1:], pf[:, 0, 1:], CLIP, None, ALU.mult).then_inc(sem["bound16"], 1)
                    dve.wait_ge(sem["bound16"], 2 * j + 1)
                    nc.vector.tensor_copy(bnd16[:, 0], bnd[:]).then_inc(sem["bound16"], 1)
                    dve.wait_ge(sem["bound16"], 2 * j + 2)
                    tt(bnd16[:, 1], bnd[:], bnd16[:, 0], ALU.subtract).then_inc(sem["bound_all"], 1)
                if s == 20 and exists(k, 1):
                    dve.wait_ge(sem["mb_ready"], j + 1)
                    b = bank("mb")
                    since(dve, "tt_done", 2 * j)
                    tt(mT[:, q], b[:, 0:P], tri, ALU.mult)
                    tsc(nbh[:], b[:, P:P + NS], -1.0, None, ALU.mult).then_inc(sem["nb16"], 1)
                    nc.vector.tensor_copy(bq[:], b[:, P:P + NS]).then_inc(sem["nb16"], 1)
                    dve.wait_ge(sem["nb16"], 3 * j + 2)
                    stt(nbl[:], b[:, P:P + NS], -1.0, nbh[:], ALU.mult, ALU.subtract).then_inc(sem["nb16"], 1)
                    for d in range(2):
                        last = tt(bqm[:, q, :, d], bq[:].rearrange("s (o n) -> s o n", o=1).broadcast_to([P, NSUB + 1, NS]),
                                  prefix.rearrange("s (j o) -> s j o", o=1).broadcast_to([P, NSUB + 1, NS]), ALU.mult)
                    last.then_inc(sem["mb_taken"], 1)
                if s in (22, 23) and exists(k, 1):
                    i = s - 22
                    half = slice(i * BANK, (i + 1) * BANK)
                    dve.wait_ge(sem["hin_ready"], 2 * j + i + 1)
                    if isinstance(k, int) and j < BATCH:
                        nc.vector.tensor_copy(h1[:, q, half], bank("hin", i)[0:NS]).then_inc(sem["hin_taken"], 1)
                    else:
                        dve.wait_ge(sem["hend_taken"], 2 * (j - 2) + i + 1)
                        stt(h1[:, q, half], h1[:, q, half], a0[:, q:q + 1], bank("hin", i)[0:NS],
                            ALU.mult, ALU.add).then_inc(sem["hin_taken"], 1)
                    dve.wait_ge(sem["hin_taken"], 2 * j + i + 1)
                    tsc(h1[:, q, half], h1[:, q, half], CLIP, -CLIP, ALU.min, ALU.max).then_inc(sem["h1_done"], 1)
                if s in (26, 27) and exists(k, 1):
                    i = s - 26
                    half = slice(i * BANK, (i + 1) * BANK)
                    dve.wait_ge(sem["carry16"], 2 * j + i + 1)
                    dve.wait_ge(sem[f"xstack_in{q}"], N_XSTACK * pair(k, p, 1))
                    stt(cc[:, half], ch[:, half], neg_low, bank("carry", i), ALU.mult, ALU.add
                        ).then_inc(sem["carry_taken"], 1)
                if s == 7 and exists(k, 0):
                    dve.wait_ge(sem["cr_ready"], k + 1)
                    since(dve, "y_ready", DB * k)
                    rep = bank("cr")[:, 0:P].rearrange("r (g e i) -> r g e i", g=4, e=4)
                    d = delta.rearrange("r (o i) -> r o i", o=1).broadcast_to([P, 4, WAYS])
                    for e in range(4):
                        last = tt(cst[:, :, e, WAYS * e:WAYS * (e + 1)], rep[:, :, e], d, ALU.mult)
                    last.then_inc(sem["cr_taken"], 1)
                if s == 13 and exists(k, -1):
                    dve.wait_ge(sem["out_ready"], k)
                    dve.wait_ge(sem["res_in"], 16 * k)
                    tt(res[:], bank("out"), res[:], ALU.add).then_inc(sem["out_taken"], 1)

            def y_copy(k, p, u):
                dve.wait_ge(sem["y_ready"], DB * k + u + 1)
                if u % 4 == 0:
                    since(dve, "yT_ready", 2 * (k - 1) + u // 4 + 1)
                cut = slice(u * P, (u + 1) * P)
                nc.vector.tensor_copy(y[:, cut], bank("y", u)[:, 0:P]).then_inc(sem["y_taken"], 1)

            def body(k, p):
                for s in range(TILES):
                    u, q = divmod(s, NQ)
                    if exists(k, 0):
                        g = TILES * k + s
                        dve.wait_ge(sem["lower_ready"], g + 1)
                        dve.wait_ge(sem["upper_copied"], g + 1)
                        since(dve, "flipped", g - 2 * NQ + 1)
                        if q == 0:
                            since(dve, "kend_done", DB * k + u - 1)
                        nc.vector.tensor_tensor_scan(ks[:, u % 2, QN * q:QN * (q + 1)].rearrange("d n t -> d (n t)"),
                                                     ps_low[:, s % 2], upper[:, s % RING], 0.0,
                                                     ALU.max, ALU.min).then_inc(sem["scanned"], 1)
                    if s in (2, 6) and exists(k, -1):
                        y_copy(k - 1, 1 - p, 6 + (s - 2) // 4)
                    if s >= 10 and s % 4 == 2 and exists(k, 0):
                        y_copy(k, p, (s - 10) // 4)
                    side(k, p, s)

            steps(dve, body)

        @block.gpsimd
        def _(pool):
            tt, tsc = nc.gpsimd.tensor_tensor, nc.gpsimd.tensor_scalar
            pool.wait_ge(sem["const_in"], N_CONST)
            pool.wait_ge(sem["halo_set"], 2)
            pool.wait_ge(sem["prep"], 1)
            pool.wait_ge(sem["rowbc_taken"], 6)

            def body(k, p):
                j, q = k + 1, (p + 1) % 2
                for s in range(TILES):
                    if s == 0 and exists(k, -1):
                        ends(k - 1, 1 - p, DB - 1)
                    if s % 4 == 0 and s >= 4 and exists(k, 0):
                        ends(k, p, s // 4 - 1)
                    if s == 1 and exists(k, 1):
                        pool.wait_ge(sem["norm_in"], j + 1)
                        since(pool, "z1", j)
                        tt(tiny[:, 1:2], tiny[:, 0:1], halfs[:, 0:1], ALU.pow).then_inc(sem["rstd"], 1)
                    if s == 7 and exists(k, 1):
                        pool.wait_ge(sem["xa"], j + 1)
                        tt(xn[:, q], xn[:, q], row_g[:], ALU.mult).then_inc(sem["xg"], 1)
                        pool.wait_ge(sem["xg"], j + 1)
                        tt(xn[:, q], xn[:, q], row_b[:], ALU.add).then_inc(sem["xn_done"], 1)
                    if s == 6 and exists(k, -1):
                        gated(k - 1, 1 - p, 1)
                    if 9 <= s < 17 and s % 2 == 1 and exists(k, 2):
                        tap = (s - 9) // 2
                        if tap == 0:
                            pool.wait_ge(sem["xr_taken"], 2 * (k + 3))
                            since(pool, "silu_done", k + 2)
                        if tap == 1:
                            since(pool, "xa", min(k + 2, STEPS) if isinstance(k, int) else k + 2)
                        dst = tapped if tap else conv[:]
                        if tap >= 2:
                            pool.wait_ge(sem["tap"], 3 * (k + 2) + tap - 1)
                        carrier(p, DB + tap)
                        for d in range(DB):
                            off = conv_b[:, p, d:d + 1] if tap == 0 else 0.0
                            last = tsc(dst[:, d, :], xr[:, p, d, tap:tap + P], cols[:, d, 3 + tap:4 + tap], off,
                                       ALU.mult, ALU.add)
                        last.then_inc(sem["tap_made"], 1)
                        pool.wait_ge(sem["tap_made"], 4 * (k + 2) + tap + 1)
                        if tap:
                            last = tt(conv[:], conv[:], tapped, ALU.add)
                            last.then_inc(sem["tap"], 1)
                            if tap == TAPS - 1:
                                nc.gpsimd.tensor_copy(xr[:, p, :, 0:TAPS - 1], xr[:, p, :, P:P + TAPS - 1]
                                                      ).then_inc(sem["conv_done"], 1)
                    if s == 12 and exists(k, 1):
                        pool.wait_ge(sem["squares"], j + 1)
                        tt(tiny[:, 5:6], tiny[:, 4:5], halfs[:, 1:2], ALU.pow).then_inc(sem["root"], 1)
                        pool.wait_ge(sem["root"], j + 1)
                        carrier(p, DB + TAPS)
                        tsc(tiny[:, 6:7], tiny[:, 5:6], 1.0, 0.0, ALU.min, ALU.max).then_inc(sem["nrm"], 1)
                        pool.wait_ge(sem["xh_done"], j + 1)
                        since(pool, f"stack_in{1 - q}", N_STACK * pair(k, p, 0))
                        tt(xl[:], xn[:, q], xh[:], ALU.subtract).then_inc(sem["xl_done"], 1)
                    if s in (2, 11) and exists(k, 0):
                        i = s // 11
                        half = slice(i * BANK, (i + 1) * BANK)
                        since(pool, "y_ready", DB * (k - 1) + 4 * (i + 1))
                        tt(dx[:, half], xn[:, p, half], row_d[:, half], ALU.mult).then_inc(sem["dx_done"], 1)
                    if s == 21 and exists(k, 1):
                        pool.wait_ge(sem["nb16"], 3 * (j + 1))
                        since(pool, f"stack_in{1 - q}", N_STACK * pair(k, p, 0))
                        m = submask.rearrange("s (o t) -> s o t", o=1).broadcast_to([P, NS, SUB])
                        for src, dst in ((nbh, tth), (nbl, ttl)):
                            tt(dst[:], src[:].rearrange("s (n o) -> s n o", o=1).broadcast_to([P, NS, SUB]), m,
                               ALU.mult).then_inc(sem["tt_done"], 1)
                    if s == 22 and exists(k, 0):
                        gated(k, p, 0)

            def carrier(p, n):
                tt(idle[:, p, n:n + 1], halfs[:, 0:1], halfs[:, 1:2], ALU.mult)

            def ends(k, p, u):
                pool.wait_ge(sem["scanned"], TILES * k + NQ * (u + 1))
                since(pool, "hend_ready", 2 * (k - 1))
                carrier(p, u)
                nc.gpsimd.tensor_copy(kend[:, p, u, :], ks[:, u % 2, :, P - 1]).then_inc(sem["kend_done"], 1)

            def gated(k, p, i):
                pool.wait_ge(sem["y_taken"], DB * k + 4 * (i + 1))
                pool.wait_ge(sem["gate_taken"], 2 * k + i + 1)
                half = slice(i * BANK, (i + 1) * BANK)
                tt(y[:, half], y[:, half], gate[:, half], ALU.mult).then_inc(sem["y_gated"], 1)

            steps(pool, body)


_OUT = "out_dram"


def kernel(x, cond_2048, L0_cond_W_in, L0_cond_W_conv, L0_cond_b_conv, L0_cond_ln_g, L0_cond_ln_b,
           L0_cond_W_xproj, L0_cond_W_dt, L0_cond_b_dt, L0_cond_A_log, L0_cond_D, L0_cond_W_out):
    import concourse.bacc as bacc
    from concourse.bass_utils import run_bass_kernel_spmd

    def col(v):
        return np.asarray(v).reshape(DB, P).T[:, :, None]

    taps = np.asarray(L0_cond_W_conv).reshape(DB, P, TAPS).transpose(1, 0, 2)
    cond = np.asarray(cond_2048).reshape(BATCH, DB, P).transpose(2, 1, 0)
    arrays = {
        "x": np.asarray(x),
        "xT": np.asarray(x).transpose(0, 2, 1),
        "xTs": np.asarray(x).reshape(BATCH, SEQ // P, P, DM)[:, :, row_steps()].reshape(BATCH, SEQ, DM
                                                                                   ).transpose(0, 2, 1),
        "w_inT": np.asarray(L0_cond_W_in).T,
        "w_outT": np.asarray(L0_cond_W_out).T,
        "wxT": np.asarray(L0_cond_W_xproj).T,
        "cols": np.concatenate([col(L0_cond_ln_g), col(L0_cond_ln_b), col(L0_cond_b_conv), taps, cond], axis=2),
        "small": np.concatenate([np.asarray(L0_cond_W_dt).T, np.zeros((NS, 2 * NS), np.float32),
                                 np.asarray(L0_cond_b_dt)[:, None],
                                 np.asarray(L0_cond_A_log)[:, None]], axis=1),
        "rows": np.stack([np.asarray(v) for v in (L0_cond_ln_g, L0_cond_ln_b, L0_cond_D)]),
        **shape_constants(),
    }
    nc = bacc.Bacc("TRN2", target_bir_lowering=False, num_devices=1)
    ins, aps = {}, {}
    for name, a in arrays.items():
        a = np.ascontiguousarray(a)
        ins[f"in_{name}"] = a
        aps[name] = nc.dram_tensor(f"in_{name}", a.shape, mybir.dt.from_np(a.dtype), kind="ExternalInput").ap()
    out = nc.dram_tensor(_OUT, (BATCH, SEQ, DM), mybir.dt.float32, kind="ExternalOutput").ap()
    scratch = nc.dram_tensor("bounds_dram", (2, NS, 2, P), mybir.dt.float16, kind="Internal").ap()
    build(nc, aps, out, scratch)
    r = run_bass_kernel_spmd(nc, [ins], core_ids=[0])
    return r.results[0][_OUT]
```

```python
import numpy as np

import concourse.bass as bass
from concourse import mybir
from contextlib import ExitStack

BATCH, SEQ, DM, DI, NS, TAPS = 2, 2048, 512, 1024, 16, 4
P = 128
DB = DI // P
CB = DM // P
STEPS = BATCH * SEQ // P
SUB = 32
NSUB = P // SUB
NQ = 4
QN = NS // NQ
WAYS = P // NS
TILES = DB * NQ
BANK = 512
CLIP = 10.0
WS = 64.0
EPS = 1e-5
RING = 2
LAG = 4


def row_steps():
    return np.arange(P).reshape(WAYS, NS).T.reshape(-1)


def shape_constants():
    s = np.arange(P)
    t = np.arange(P)
    step = row_steps()
    tri = ((s[:, None] <= step[None, :]) & (s[:, None] >= 1)).astype(np.float32)
    shuffle = (t[:, None] == step[None, :]).astype(np.float32)
    r = np.arange(SUB)
    sub = ((r[:, None] <= r[None, :]) & (r[:, None] >= 1)).astype(np.float32)
    sub = np.tile(sub, (NSUB, 1))
    heads = np.array([SUB * jj for jj in range(NSUB)] + [P - 1])
    prefix = ((s[:, None] <= heads[None, :]) & (s[:, None] >= 1)).astype(np.float32)
    delta = np.tile(np.eye(WAYS, dtype=np.float32), (NS, 1))
    low = np.where((s % SUB) >= NS, -1.0, 0.0).astype(np.float32)[:, None]
    c128 = np.concatenate([np.eye(P, dtype=np.float32), tri, shuffle, sub, prefix, delta, low], axis=1)
    twice = np.tile(np.eye(NS, dtype=np.float32), (1, P // NS))
    twice[:, SUB:] = 0.0
    spread = np.repeat(np.eye(NS, dtype=np.float32), WAYS, axis=1)
    c16 = np.concatenate([twice, spread], axis=1)
    carry = np.zeros((2, NS, NSUB, 2, NS, SUB), np.float16)
    for n in range(NS):
        carry[:, n, 1:, :, n, :] = -1.0
        carry[:, n, 0, :, n, 0] = 1.0
    ones = np.ones((1, NSUB * DI), np.float16)
    return {"c128": c128, "c16": c16, "carry": carry.reshape(2 * NS, -1), "ones16": ones}


SEMS = """
xT_in xs_in xT_high xT_low xs_high xs_low w_piece0 w_piece1 w_high w_low res_in out_done0 out_done1 const_in
xstack_in0 xstack_in1 stack_in0 stack_in1 bound_out bound_in0 bound_in1
rows_ready ones_ready gw_ready sums_ready sums_taken halo_set prep rowbc_ready rowbc_taken p16 act_prep
lower_ready upper_ready upper_copied scanned flipped flip_copied
xr_ready xr_taken xt_ready xt_taken z_ready z_taken zT_ready zT_taken dt_ready dt_taken
mb_ready mb_taken cr_ready cr_taken hin_ready hin_taken carry_ready carry_taken
hend_ready hend_taken y_ready y_taken yT_ready yT_taken gate_ready gate_taken
out_ready out_taken
conv_done tap tap_made silu_done stats aggr rstd moments z1 zb ad scan_p recip weighted bound16 bound_all
norm_in xa xg xn_done xh_done xl_done yT_high squares root nrm nb16 tt_done dx_done kend_done y_gated h1_done
carry16
""".split()


def build(nc, A, out, scratch):
    F, H = mybir.dt.float32, mybir.dt.float16
    ALU, ACT = mybir.AluOpType, mybir.ActivationFunctionType
    with ExitStack() as S:
        def sb(name, shape, dt=F):
            return S.enter_context(nc.sbuf_tensor(name, shape, dt))

        sem = {n: S.enter_context(nc.semaphore(n)) for n in SEMS}

        w_in = sb("w_in", [P, 2, CB, 2 * DI], H)
        w_out = sb("w_out", [P, 2, DB, DM], H)
        c128 = sb("c128_sb", [P, 3 * P + SUB + NSUB + 1 + WAYS + 1])
        at = 0
        parts = []
        for width in (P, P, P, SUB, NSUB + 1, WAYS, 1):
            parts.append(c128[:, at:at + width])
            at += width
        ident, tri, shuffle, submask, prefix, delta, neg_low = parts
        c16 = sb("c16_sb", [NS, 2 * P])
        twice = c16[:, 0:P]
        spread = c16[:, P:2 * P]
        cols = sb("cols_sb", [P, DB, 3 + TAPS + BATCH])
        small = sb("small_sb", [NS, 3 * NS + 2])
        row_g = sb("row_g", [P, DI])
        row_b = sb("row_b", [P, DI])
        row_d = sb("row_d", [P, DI])
        gw = sb("gw", [P, DB, 3 * NS])
        sums = sb("sums", [P, 2, 3 * NS])
        conv_b = sb("conv_b", [P, BATCH, DB])
        a01 = sb("a01", [NS, 2])
        halfs = sb("halfs", [P, 2])
        idle = sb("idle", [P, 2, 2 * TAPS + 1])
        zeros = sb("zeros", [NS, P])

        xf = sb("xf", [P, CB, P])
        x16 = sb("x16", [P, 2, CB, P], H)
        xr = sb("xr", [P, BATCH, DB, TAPS - 1 + P])
        conv = sb("conv", [P, DB, P])
        xcT = sb("xcT", [P, DB, P])
        yT = xcT[:].rearrange("d c t -> d (c t)").bitcast(H).rearrange("d (h c t) -> d h c t", h=2, c=DB)
        xc = sb("xc", [P, DI])
        tapped = xc[:].rearrange("d (c t) -> d c t", c=DB)
        wx = conv[:, :, 0:3 * NS]
        bw = conv[:, :, 3 * NS:6 * NS] if 6 * NS <= P else tapped[:, :, 0:3 * NS]
        ws = sb("ws", [P, 5, DB])
        xn = sb("xn", [P, 2, DI])
        xh = sb("xh", [P, DI], H)
        xl = sb("xl", [P, DI], H)
        st = sb("st", [P, 2, 6])
        mom = sb("mom", [P, 2])
        tiny = sb("tiny", [P, 8])

        z = sb("z", [P, 3 * NS])
        z1 = sb("z1", [P, 3 * NS])
        z2 = sb("z2", [P, 3 * NS])
        zT = sb("zT", [NS, 3, P])
        th = sb("th", [NS, P])
        ad = sb("ad", [NS, P])
        a0 = sb("a0", [NS, 2])
        pf = sb("pf", [NS, 2, P])
        p_end = sb("p_end", [NS, 2])
        bc = sb("bc", [NS, 2, 2, P])
        bnd = sb("bnd", [NS, 2, P])
        bnd16 = sb("bnd16", [NS, 2, 2, P], H)
        mT = sb("mT", [P, 2, P])
        nbh = sb("nbh", [P, NS], H)
        nbl = sb("nbl", [P, NS], H)
        bq = sb("bq", [P, NS])
        bqm = sb("bqm", [P, 2, NSUB + 1, 2, NS])
        cst = sb("cst", [P, 4, 4, SUB])
        tth = sb("tth", [P, NS, SUB], H)
        ttl = sb("ttl", [P, NS, SUB], H)
        h1 = sb("h1", [NS, 2, DI])
        ch = xh
        cc = xl

        xs = sb("xs", [P, 2, NSUB, DI], H)
        ts = sb("ts", [P, 2, NSUB, 2, NS * SUB], H)

        upper = sb("upper", [P, RING, BANK])
        ks = sb("ks", [P, 2, NS, P])
        kend = sb("kend", [P, 2, DB, NS])
        kT = sb("kT", [P, 2, 4, 4, P])

        gate = sb("gate", [P, DI])
        y = sb("y", [P, DI])
        ones = y[:, 0:P]
        dx = sb("dx", [P, DI])
        res = sb("res", [P, DM])

        ps_low = S.enter_context(nc.psum_tensor("ps_low", [P, 2, BANK], F))
        ps_up = S.enter_context(nc.psum_tensor("ps_up", [P, 2, BANK], F))
        ps_flip = S.enter_context(nc.psum_tensor("ps_flip", [P, 2, BANK], F))
        ps_job = S.enter_context(nc.psum_tensor("ps_job", [P, 2, BANK], F))

        def since(eng, name, value):
            if isinstance(value, int) and value <= 0:
                return
            eng.wait_ge(sem[name], value)

        JOBS = [(0, 1, "z", 0, 1, 1), (2, 2, "y", 6, -1, 8), (4, 1, "yT", 0, -1, 2),
                (5, 4, "gate", 0, 0, 2), (10, 2, "y", 7, -1, 8), (12, 2, "hend", 0, -1, 2),
                (14, 1, "cr", 0, 0, 1), (15, 2, "hend", 1, -1, 2), (17, 4, "gate", 1, 0, 2),
                (21, 1, "yT", 1, -1, 2), (22, 2, "y", 0, 0, 8), (24, 5, "out", 0, -1, 1),
                (29, 1, "zT", 0, 1, 1), (30, 2, "y", 1, 0, 8), (32, 1, "dt", 0, 1, 1),
                (33, 4, "xr", 0, 2, 2), (37, 2, "y", 2, 0, 8), (39, 1, "mb", 0, 1, 1),
                (40, 4, "xr", 1, 2, 2), (44, 2, "y", 3, 0, 8), (46, 1, "hin", 0, 1, 2),
                (47, 1, "hin", 1, 1, 2), (49, 2, "carry", 0, 1, 2), (51, 2, "y", 4, 0, 8),
                (53, 2, "carry", 1, 1, 2), (56, 1, "xt", 0, 2, 2), (58, 2, "y", 5, 0, 8),
                (60, 1, "xt", 1, 2, 2)]
        assert len(JOBS) % 2 == 0
        LAST = {(name, i): first + parts - 1 for first, parts, name, i, _, _ in JOBS}
        BANK_OF = {(name, i): m % 2 for m, (_, _, name, i, _, _) in enumerate(JOBS)}

        def exists(k, off):
            return not isinstance(k, int) or 0 <= k + off < STEPS

        def bank_free(pe, k, m):
            kk, mm = k, m
            while True:
                mm -= 2
                if mm < 0:
                    mm += len(JOBS)
                    kk = kk - 1
                    if isinstance(kk, int) and kk < -2:
                        return
                _, _, name, i, off, per = JOBS[mm]
                if exists(kk, off):
                    pe.wait_ge(sem[name + "_taken"], (kk + off) * per + i + 1)
                    return

        def steps(eng, body):
            for k in range(-2, 2):
                body(k, k % 2)
            with eng.Fori(2, STEPS - 2, 2) as k0:
                body(k0, 0)
                body(k0 + 1, 1)
            for k in range(STEPS - 2, STEPS + 1):
                body(k, k % 2)

        staged = [ks[:, h].rearrange("p n t -> p (n t)") for h in range(2)]
        w_in_dram = A["w_inT"].rearrange("(c p) d -> p c d", p=P)
        w_out_dram = A["w_outT"].rearrange("(h c p) d -> p h c d", p=P, h=2)
        pieces = [(w_in_dram[:, c], w_in[:, 0, c], w_in[:, 1, c]) for c in range(CB)]
        for g in range(2):
            part = slice(g * DB // 2, (g + 1) * DB // 2)
            pieces.append((w_out_dram[:, g], w_out[:, 0, part], w_out[:, 1, part]))

        def staged_like(n, piece):
            flat = staged[n % 2]
            return flat if len(piece.shape) == 2 else flat.rearrange("p (c d) -> p c d", d=piece.shape[2])

        block = S.enter_context(nc.Block())

        @block.sync
        def _(sp):
            loads = [(c128[:], A["c128"]), (c16[:], A["c16"]),
                     (cols[:], A["cols"]), (wx, A["wxT"].rearrange("(c p) m -> p c m", p=P)),
                     (small[:], A["small"]),
                     (row_g[0:1], A["rows"][0:1]), (row_b[0:1], A["rows"][1:2]), (row_d[0:1], A["rows"][2:3])]
            for p in range(2):
                carry = A["carry"].rearrange("r (j c) -> r j c", j=NSUB)
                loads.append((ts[96:128, p].rearrange("r j v c -> r j (v c)"), carry))
                for r in (0, 32):
                    loads.append((xs[r:r + 1, p], A["ones16"].rearrange("o (j d) -> o j d", j=NSUB)))
            for dst, src in loads:
                sp.dma_start(dst, src).then_inc(sem["const_in"], 16)
            for n, (src, _, _) in enumerate(pieces):
                since(sp, "w_high", n - 1)
                since(sp, "w_low", n - 1)
                sp.dma_start(staged_like(n, src), src).then_inc(sem[f"w_piece{n % 2}"], 16)

            xT_dram = A["xT"].rearrange("b (c p) t -> b p c t", p=P)
            xTs_dram = A["xTs"].rearrange("b (c p) t -> b p c t", p=P)
            x_dram = A["x"]

            def body(k, p):
                def chunk(off):
                    b = (p + off) % 2
                    c = (k + off - b) // 2 if isinstance(k, int) else (k + (off - b)) // 2
                    return b, c

                if exists(k, 2):
                    b, c = chunk(2)
                    before = ("xs_high", "xs_low")
                    if isinstance(k, int) and k == -1:
                        before = ("xT_high", "xT_low")
                    for name in before:
                        since(sp, name, max(k + 1, 1) if isinstance(k, int) and k == -1 else k + 1)
                    sp.dma_start(xf[:], xT_dram[b, :, :, bass.ds(c * P, P)]).then_inc(sem["xT_in"], 16)
                if exists(k, -1):
                    b, c = chunk(-1)
                    if not (isinstance(k, int) and k < 2):
                        sp.wait_ge(sem[f"out_done{p}"], 16 * ((k - p) // 2))
                    sp.dma_start(res[:], x_dram[b, bass.ds(c * P, P), :]).then_inc(sem["res_in"], 16)
                if exists(k, 1):
                    j, pn = k + 1, (p + 1) % 2
                    xstack, stack = sem[f"xstack_in{pn}"], sem[f"stack_in{pn}"]
                    since(sp, "upper_ready", TILES * k)
                    sp.wait_ge(sem["xh_done"], j + 1)
                    for jj in range(NSUB):
                        a = SUB * jj
                        sp.dma_start(xs[1:SUB, pn, jj], xh[a + 1:a + SUB]).then_inc(xstack, 16)
                        sp.dma_start(xs[SUB + 1:2 * SUB, pn, jj], xh[a + 1:a + SUB]).then_inc(xstack, 16)
                    sp.wait_ge(sem["xl_done"], j + 1)
                    for jj in range(NSUB):
                        a = SUB * jj
                        sp.dma_start(xs[2 * SUB:3 * SUB, pn, jj], xl[a:a + SUB]).then_inc(xstack, 16)
                    b, c = chunk(1)
                    if exists(k, 2):
                        sp.wait_ge(sem["xT_high"], k + 3)
                        sp.wait_ge(sem["xT_low"], k + 3)
                    else:
                        sp.wait_ge(sem["xs_low"], k + 1)
                        sp.wait_ge(sem["xs_high"], k + 1)
                    sp.dma_start(xf[:], xTs_dram[b, :, :, bass.ds(c * P, P)]).then_inc(sem["xs_in"], 16)
                if exists(k, -1):
                    b, c = chunk(-1)
                    sp.wait_ge(sem["out_taken"], k)
                    sp.dma_start(out[b, bass.ds(c * P, P), :], res[:]).then_inc(sem[f"out_done{b}"], 16)
                if exists(k, 1):
                    sp.wait_ge(sem["bound_all"], j + 1)
                    for h in range(2):
                        for v in range(2):
                            sp.dma_start(scratch[h, :, v].rearrange("j n t -> n j t"),
                                         bnd16[:, h, v].rearrange("n (j t) -> n j t", j=NSUB)
                                         ).then_inc(sem["bound_out"], 16)
                    sp.wait_ge(sem["bound_out"], 64 * (j + 1))
                    for h in range(2):
                        sp.dma_start(ts[SUB * h:SUB * h + 1, pn].rearrange("o j v c -> o (j v c)"),
                                     scratch[h].rearrange("(o j) v n t -> o (j v n t)", o=1)
                                     ).then_inc(sem[f"bound_in{pn}"], 16)
                    sp.wait_ge(sem["tt_done"], 2 * (j + 1))
                    for jj in range(NSUB):
                        a = SUB * jj
                        for r, half in ((0, tth), (SUB, ttl), (2 * SUB, tth)):
                            lead = 0 if r == 2 * SUB else 1
                            rows = half[a + lead:a + SUB].rearrange("s (o n) t -> s o (n t)", o=1)
                            sp.dma_start(ts[r + lead:r + SUB, pn, jj],
                                         rows.broadcast_to([SUB - lead, 2, NS * SUB])).then_inc(stack, 16)
                    sp.wait_ge(sem["carry_taken"], 2 * j + 2)
                    for jj in range(NSUB):
                        sp.dma_start(xs[3 * SUB:P, pn, jj], cc[SUB * jj:SUB * jj + SUB]).then_inc(stack, 16)

            steps(sp, body)
            for b in range(BATCH):
                sp.wait_ge(sem[f"out_done{b}"], 16 * (STEPS // BATCH))
            sp.wait_ge(sem["bound_out"], 64 * STEPS)

        N_CONST = 16 * 14
        N_XSTACK = 16 * 3 * NSUB
        N_STACK = 16 * (3 * NSUB + NSUB)
        N_BOUND = 16 * 2

        def pair(k, p, off):
            q = (p + off) % 2
            return (k + off - q) // 2 + 1

        @block.tensor
        def _(pe):
            mm = nc.tensor.matmul
            tr = nc.tensor.transpose
            pe.wait_ge(sem["const_in"], N_CONST)
            pe.wait_ge(sem["prep"], 1)
            for i, row in enumerate((row_g, row_b, row_d)):
                for h in range(2):
                    n = 2 * i + h
                    if n >= 2:
                        pe.wait_ge(sem["rowbc_taken"], n - 1)
                    mm(ps_job[:, n % 2], ones[0:1, :], row[0:1, h * BANK:(h + 1) * BANK],
                       start=True, stop=True).then_inc(sem["rowbc_ready"], 1)
            pe.wait_ge(sem["gw_ready"], 2)
            for i, src in enumerate((gw, bw)):
                for c in range(DB):
                    last = mm(ps_up[:, i, 0:3 * NS], ones, src[:, c], start=(c == 0), stop=(c == DB - 1))
                last.then_inc(sem["sums_ready"], 1)
            pe.wait_ge(sem["sums_taken"], 1)
            pe.wait_ge(sem["rowbc_taken"], 6)
            pe.wait_ge(sem["w_low"], len(pieces))
            pe.wait_ge(sem["w_high"], len(pieces))
            PASSES = ((0, 0), (0, 1), (1, 0))

            def job(k, p, m, part):
                _, parts, name, i, off, per = JOBS[m]
                if not exists(k, off):
                    return
                j = k + off
                q = (p + off) % 2
                ps = ps_job[:, m % 2]
                ready = sem[name + "_ready"]
                half = slice(i * BANK, (i + 1) * BANK)
                if part == 0:
                    inputs(j, q, name, i)
                    bank_free(pe, k, m)

                def share(n):
                    return range(part * n // parts, (part + 1) * n // parts)

                if name == "xr":
                    for e in share(4):
                        d = (4 * i + e) * P
                        for c in range(CB):
                            for n, (a, b) in enumerate(PASSES):
                                last = mm(ps[:, e * P:(e + 1) * P], w_in[:, a, c, d:d + P], x16[:, b, c, :],
                                          start=(c == n == 0), stop=(c == CB - 1 and n == 2))
                elif name == "gate":
                    for c in share(CB):
                        for n, (a, b) in enumerate(PASSES):
                            last = mm(ps, x16[:, a, c, :], w_in[:, b, c, DI + i * BANK:DI + (i + 1) * BANK],
                                      start=(c == n == 0), stop=(c == CB - 1 and n == 2))
                elif name == "xt":
                    for e in range(4):
                        last = tr(ps[:, e * P:(e + 1) * P], xcT[:, 4 * i + e, :], ident)
                elif name == "z":
                    for c in range(DB):
                        last = mm(ps[:, 0:3 * NS], xcT[:, c, :], gw[:, c, :], start=(c == 0), stop=(c == DB - 1))
                elif name == "zT":
                    for e in range(3):
                        last = tr(ps[0:NS, e * P:(e + 1) * P], z[:, e * NS:(e + 1) * NS], ident)
                elif name == "dt":
                    last = mm(ps[0:3 * NS, 0:P], small[:, 0:3 * NS], zT[:, 2, :], start=True, stop=True)
                elif name == "mb":
                    mm(ps[:, 0:P], bc[:, q, 0, :], bc[:, q, 1, :], start=True, stop=True)
                    last = tr(ps[:, P:P + NS], bc[:, q, 0, :], ident[0:NS, 0:NS])
                elif name == "cr":
                    last = mm(ps[:, 0:P], spread, bc[:, q, 1, :], start=True, stop=True)
                elif name == "hin":
                    last = mm(ps[0:3 * NS], z[0:1, :], xn[0:1, q, half], start=True, stop=True)
                elif name == "carry":
                    if part == 0:
                        mm(ps, twice, h1[:, q, half], start=True, stop=False)
                    if part == parts - 1:
                        last = mm(ps, bqm[:, q, 0:NSUB].rearrange("s j d n -> s (j d n)"), xn[:, q, half],
                                  start=False, stop=True)
                elif name == "hend":
                    if part == 0:
                        mm(ps[0:NS], bqm[:, q, NSUB, 0, :], xn[:, q, half], start=True, stop=False)
                    if part == parts - 1:
                        for e in range(4):
                            last = mm(ps[0:NS, e * P:(e + 1) * P], kend[:, q, 4 * i + e, :], ident,
                                      start=False, stop=(e == 3))
                elif name == "y":
                    if part == 0:
                        mm(ps[:, 0:P], mT[:, q, :], xn[:, q, i * P:(i + 1) * P], start=True, stop=False)
                        mm(ps[:, 0:P], shuffle, dx[:, i * P:(i + 1) * P], start=False, stop=False)
                    for e in share(4):
                        for g in range(4):
                            last = mm(ps[SUB * g:SUB * (g + 1), 0:P], cst[:, g, e, :], kT[:, i % 2, g, e, :],
                                      start=False, stop=(e == 3))
                elif name == "yT":
                    for e in range(4):
                        d = 4 * i + e
                        last = tr(ps[:, e * P:(e + 1) * P], y[:, d * P:(d + 1) * P], ident)
                elif name == "out":
                    for c in share(DB):
                        for n, (a, b) in enumerate(PASSES):
                            last = mm(ps, yT[:, a, c, :], w_out[:, b, c, :], start=(c == n == 0),
                                      stop=(c == DB - 1 and n == 2))
                if part == parts - 1:
                    last.then_inc(ready, 1)

            def inputs(j, q, name, i):
                if name == "xr":
                    pe.wait_ge(sem["xT_high"], j + 1)
                    pe.wait_ge(sem["xT_low"], j + 1)
                elif name == "gate":
                    pe.wait_ge(sem["xs_high"], j + 1)
                    pe.wait_ge(sem["xs_low"], j + 1)
                elif name == "xt":
                    pe.wait_ge(sem["silu_done"], 2 * j + i + 1)
                elif name == "z":
                    pe.wait_ge(sem["silu_done"], 2 * (j + 1))
                elif name == "zT":
                    pe.wait_ge(sem["zb"], j + 1)
                elif name == "dt":
                    pe.wait_ge(sem["zT_taken"], j + 1)
                elif name in ("mb", "cr"):
                    pe.wait_ge(sem["weighted"], j + 1)
                elif name == "hin":
                    pe.wait_ge(sem["zb"], j + 1)
                    pe.wait_ge(sem["xn_done"], j + 1)
                elif name == "carry":
                    pe.wait_ge(sem["mb_taken"], j + 1)
                    pe.wait_ge(sem["h1_done"], 2 * j + i + 1)
                elif name == "hend":
                    pe.wait_ge(sem["kend_done"], DB * (j + 1))
                elif name == "y":
                    pe.wait_ge(sem["flip_copied"], TILES * j + NQ * (i + 1))
                    if i == 0:
                        pe.wait_ge(sem["cr_taken"], j + 1)
                    if i % 4 == 0:
                        pe.wait_ge(sem["dx_done"], 2 * j + i // 4 + 1)
                elif name == "yT":
                    pe.wait_ge(sem["y_gated"], 2 * j + i + 1)
                elif name == "out":
                    pe.wait_ge(sem["yT_taken"], 2 * (j + 1))

            def fill(k, p, s):
                g = TILES * k + s
                u, q = divmod(s, NQ)
                if s == 0:
                    pe.wait_ge(sem[f"xstack_in{p}"], N_XSTACK * pair(k, p, 0))
                    pe.wait_ge(sem[f"stack_in{p}"], N_STACK * pair(k, p, 0))
                    pe.wait_ge(sem[f"bound_in{p}"], N_BOUND * pair(k, p, 0))
                for v, ps, free, ready in ((1, ps_up, "upper_copied", "upper_ready"),
                                           (0, ps_low, "scanned", "lower_ready")):
                    since(pe, free, g - 1)
                    o = ps[:, s % 2].rearrange("d (n t) -> d n t", n=QN)
                    for jj in range(NSUB):
                        last = mm(o[:, :, SUB * jj:SUB * (jj + 1)], xs[:, p, jj, u * P:(u + 1) * P],
                                  ts[:, p, jj, v, q * QN * SUB:(q + 1) * QN * SUB].rearrange("s (n t) -> s n t", n=QN),
                                  start=True, stop=True)
                    last.then_inc(sem[ready], 1)

            def flip(k, p, s):
                g = TILES * k + s
                u, q = divmod(s, NQ)
                if q == 0:
                    pe.wait_ge(sem["scanned"], g + NQ)
                since(pe, "flip_copied", g - 1)
                flat = ks[:, u % 2].rearrange("d n t -> d (n t)")
                for e in range(4):
                    last = tr(ps_flip[:, s % 2, e * P:(e + 1) * P], flat[:, bass.ds(4 * q + e, P, step=NS)], ident)
                last.then_inc(sem["flipped"], 1)

            def jobs_at(k, p, point):
                for m, (first, parts, *_) in enumerate(JOBS):
                    if first <= point < first + parts:
                        job(k, p, m, point - first)

            def body(k, p):
                for s in range(TILES):
                    if exists(k, 0) and s == 0:
                        fill(k, p, 0)
                    if exists(k, 0) and s + 1 < TILES:
                        fill(k, p, s + 1)
                    jobs_at(k, p, 2 * s)
                    t = s - LAG
                    if t >= 0 and exists(k, 0):
                        flip(k, p, t)
                    elif t < 0 and exists(k, -1):
                        flip(k - 1, 1 - p, t + TILES)
                    jobs_at(k, p, 2 * s + 1)

            steps(pe, body)

        @block.scalar
        def _(act):
            copy, act_fn = nc.scalar.copy, nc.scalar.activation
            act.wait_ge(sem["const_in"], N_CONST)
            act_fn(tiny[:, 7:8], cols[:, 0, 0:1], ACT.Silu).then_inc(sem["act_prep"], 1)
            act_fn(a01[:, 0:1], small[:, 3 * NS + 1:3 * NS + 2], ACT.Tanh).then_inc(sem["act_prep"], 1)
            for i, row in enumerate((row_g, row_b, row_d)):
                for h in range(2):
                    n = 2 * i + h
                    act.wait_ge(sem["rowbc_ready"], n + 1)
                    if h:
                        act.wait_ge(sem["rowbc_ready"], n + 1)
                    copy(row[:, h * BANK:(h + 1) * BANK], ps_job[:, n % 2]).then_inc(sem["rowbc_taken"], 1)
            act.wait_ge(sem["sums_ready"], 2)
            copy(sums[:], ps_up[:, :, 0:3 * NS]).then_inc(sem["sums_taken"], 1)
            for n, (_, high, _) in enumerate(pieces):
                act.wait_ge(sem[f"w_piece{n % 2}"], 16 * (n // 2 + 1))
                act_fn(high, staged_like(n, high), ACT.Identity, scale=WS).then_inc(sem["w_high"], 1)

            def bank(name, i=0):
                return ps_job[:, BANK_OF[name, i]]

            def side(k, p, point):
                def take(name, i, off, per):
                    act.wait_ge(sem[name + "_ready"], (k + off) * per + i + 1)

                def at(name, off, per=2):
                    return [i for i in range(per) if LAST[name, i] == point and exists(k, off)]

                for i in at("hend", -1):
                    q = (p + 1) % 2
                    take("hend", i, -1, 2)
                    act_fn(h1[:, q, i * BANK:(i + 1) * BANK], bank("hend", i)[0:NS], ACT.Identity,
                           scale=p_end[:, q:q + 1]).then_inc(sem["hend_taken"], 1)
                if point == 17 and exists(k, 1):
                    j, q = k + 1, (p + 1) % 2
                    act.wait_ge(sem["moments"], j + 1)
                    act.wait_ge(sem["xt_taken"], 2 * (j + 1))
                    since(act, "y_ready", DB * k)
                    since(act, "hend_ready", 2 * k)
                    act_fn(xn[:, q], xc[:], ACT.Identity, scale=tiny[:, 1:2],
                           bias=tiny[:, 3:4]).then_inc(sem["xa"], 1)
                for i in at("yT", -1):
                    take("yT", i, -1, 2)
                    since(act, "z_ready", min(k + 2, STEPS) if isinstance(k, int) else k + 2)
                    copy(yT[:, 0, 4 * i:4 * i + 4, :],
                         bank("yT", i).rearrange("d (e t) -> d e t", e=4)).then_inc(sem["yT_high"], 1)
                for i in at("gate", 0):
                    take("gate", i, 0, 2)
                    since(act, "y_gated", 2 * (k - 1) + i + 1)
                    act_fn(gate[:, i * BANK:(i + 1) * BANK], bank("gate", i), ACT.Silu, scale=1 / WS
                           ).then_inc(sem["gate_taken"], 1)
                if point == 23 and exists(k, 1):
                    j, q = k + 1, (p + 1) % 2
                    act.wait_ge(sem["xn_done"], j + 1)
                    since(act, "carry_taken", 2 * j)
                    act_fn(ch[:], xn[:, q], ACT.Square, accum_out=tiny[:, 4:5]).then_inc(sem["squares"], 1)
                    act.wait_ge(sem["squares"], j + 1)
                    act_fn(xh[:], xn[:, q], ACT.Identity).then_inc(sem["xh_done"], 1)
                if point == 25 and exists(k, 2):
                    act.wait_ge(sem["xT_in"], 16 * (k + 3))
                    since(act, "gate_ready", 2 * (k + 1))
                    if isinstance(k, int) and k == -1:
                        act.wait_ge(sem["xr_ready"], 2)
                    copy(x16[:, 0], xf[:]).then_inc(sem["xT_high"], 1)
                for _ in at("zT", 1, 1):
                    take("zT", 0, 1, 1)
                    copy(zT[:], bank("zT")[0:NS, 0:3 * P].rearrange("n (e t) -> n e t", e=3)
                         ).then_inc(sem["zT_taken"], 1)
                for _ in at("dt", 1, 1):
                    take("dt", 0, 1, 1)
                    act_fn(th[:], bank("dt")[0:NS, 0:P], ACT.Tanh, bias=small[:, 3 * NS:3 * NS + 1]
                           ).then_inc(sem["dt_taken"], 1)
                for i in at("xr", 2):
                    take("xr", i, 2, 2)
                    since(act, "conv_done", 2 * (k + 1) + i + 1)
                    act_fn(xr[:, p, 4 * i:4 * i + 4, TAPS - 1:], bank("xr", i).rearrange("d (e t) -> d e t", e=4),
                           ACT.Identity, scale=1 / WS).then_inc(sem["xr_taken"], 1)
                if point == 46 and exists(k, 1):
                    act.wait_ge(sem["xs_in"], 16 * (k + 2))
                    since(act, "xr_ready", min(2 * (k + 3), 2 * STEPS) if isinstance(k, int) else 2 * (k + 3))
                    since(act, "gate_ready", 2 * (k + 1))
                    copy(x16[:, 0], xf[:]).then_inc(sem["xs_high"], 1)
                if point in (49, 57) and exists(k, 2):
                    i = (point - 49) // 8
                    part = slice(4 * i, 4 * i + 4)
                    act.wait_ge(sem["tap"], 6 * (k + 2) + 3 * (i + 1))
                    since(act, "z_ready", min(k + 2, STEPS) if isinstance(k, int) else k + 2)
                    since(act, "out_ready", k)
                    act_fn(xcT[:, part], conv[:, part], ACT.Silu).then_inc(sem["silu_done"], 1)
                for i in at("xt", 2):
                    take("xt", i, 2, 2)
                    since(act, "xa", k + 2)
                    copy(xc[:, i * BANK:(i + 1) * BANK], bank("xt", i)).then_inc(sem["xt_taken"], 1)
                for i in at("carry", 1):
                    take("carry", i, 1, 2)
                    act.wait_ge(sem[f"xstack_in{1 - p}"], N_XSTACK * pair(k, p, 1))
                    copy(ch[:, i * BANK:(i + 1) * BANK], bank("carry", i)).then_inc(sem["carry16"], 1)

            def copy_flip(k, p, s):
                g = TILES * k + s
                u, q = divmod(s, NQ)
                act.wait_ge(sem["flipped"], g + 1)
                since(act, "y_ready", DB * k + u - 1)
                copy(kT[:, u % 2, q], ps_flip[:, s % 2].rearrange("r (e d) -> r e d", e=4)
                     ).then_inc(sem["flip_copied"], 1)

            def body(k, p):
                def copy_upper(s):
                    g = TILES * k + s
                    act.wait_ge(sem["upper_ready"], g + 1)
                    since(act, "scanned", g - RING + 1)
                    copy(upper[:, s % RING], ps_up[:, s % 2]).then_inc(sem["upper_copied"], 1)

                for s in range(TILES):
                    if exists(k, 0) and s == 0:
                        copy_upper(0)
                    if exists(k, 0) and s + 1 < TILES:
                        copy_upper(s + 1)
                    side(k, p, 2 * s)
                    t = s - LAG
                    if t >= 0 and exists(k, 0):
                        copy_flip(k, p, t)
                    elif t < 0 and exists(k, -1):
                        copy_flip(k - 1, 1 - p, t + TILES)
                    side(k, p, 2 * s + 1)

            steps(act, body)

        @block.vector
        def _(dve):
            tt, tsc, stt = nc.vector.tensor_tensor, nc.vector.tensor_scalar, nc.vector.scalar_tensor_tensor
            nc.vector.memset(ones, 1.0)
            nc.vector.memset(zeros[:], 0.0)
            nc.vector.memset(halfs[:, 0:1], -0.5)
            nc.vector.memset(halfs[:, 1:2], 0.5)
            nc.vector.memset(pf[:, 1, 0:1], 1.0)
            nc.vector.memset(cst[:], 0.0)
            nc.vector.memset(bqm[:], 0.0).then_inc(sem["prep"], 1)
            dve.wait_ge(sem["const_in"], N_CONST)
            tt(gw[:], wx, cols[:, :, 0:1].broadcast_to([P, DB, 3 * NS]), ALU.mult).then_inc(sem["gw_ready"], 1)
            tt(bw, wx, cols[:, :, 1:2].broadcast_to([P, DB, 3 * NS]), ALU.mult).then_inc(sem["gw_ready"], 1)
            tap0 = 3
            tt(ws[:, 0, :], cols[:, :, tap0], cols[:, :, tap0 + 1], ALU.add).then_inc(sem["p16"], 1)
            tt(ws[:, 1, :], cols[:, :, tap0 + 2], cols[:, :, tap0 + 3], ALU.add).then_inc(sem["p16"], 1)
            dve.wait_ge(sem["p16"], 2)
            tt(ws[:, 2, :], ws[:, 0, :], ws[:, 1, :], ALU.add).then_inc(sem["p16"], 1)
            dve.wait_ge(sem["p16"], 3)
            for b in range(BATCH):
                cond = cols[:, :, 3 + TAPS + b]
                tt(ws[:, 3 + b, :], ws[:, 2, :], cond, ALU.mult).then_inc(sem["p16"], 1)
                dve.wait_ge(sem["p16"], 4 + b)
                tt(conv_b[:, b, :], ws[:, 3 + b, :], cols[:, :, 2], ALU.add)
                tsc(xr[:, b, :, 0:TAPS - 1],
                    cols[:, :, 3 + TAPS + b:4 + TAPS + b].broadcast_to([P, DB, TAPS - 1]),
                    -1.0, None, ALU.mult).then_inc(sem["halo_set"], 1)
            dve.wait_ge(sem["act_prep"], 2)
            tsc(a01[:, 1:2], a01[:, 0:1], -0.01, None, ALU.mult).then_inc(sem["p16"], 1)
            dve.wait_ge(sem["p16"], 6)
            for n, (_, high, low) in enumerate(pieces):
                dve.wait_ge(sem["w_high"], n + 1)
                stt(low, staged_like(n, low), WS, high, ALU.mult, ALU.subtract).then_inc(sem["w_low"], 1)

            def bank(name, i=0):
                return ps_job[:, BANK_OF[name, i]]

            def side(k, p, point):
                j, q = k + 1, (p + 1) % 2
                if point == 0 and exists(k, 1):
                    dve.wait_ge(sem["xt_taken"], 2 * (j + 1))
                    nc.vector.bn_stats(st[:, 0], xc[:, 0:BANK]).then_inc(sem["stats"], 1)
                    nc.vector.bn_stats(st[:, 1], xc[:, BANK:]).then_inc(sem["stats"], 1)
                    dve.wait_ge(sem["stats"], 2 * (j + 1))
                    since(dve, "xa", j)
                    nc.vector.memset(tiny[:, 7:8], 0.0)
                    nc.vector.bn_aggr(mom[:], st[:].rearrange("p a b -> p (a b)")).then_inc(sem["aggr"], 1)
                    dve.wait_ge(sem["aggr"], j + 1)
                    tsc(tiny[:, 0:1], mom[:, 1:2], EPS, None, ALU.add)
                    tsc(tiny[:, 2:3], mom[:, 0:1], -1.0, None, ALU.mult).then_inc(sem["norm_in"], 1)
                if point == 2 and exists(k, 1):
                    dve.wait_ge(sem["norm_in"], j + 1)
                    dve.wait_ge(sem["z_ready"], j + 1)
                    stt(z1[:], sums[:, 0, :], tiny[:, 2:3], bank("z")[:, 0:3 * NS], ALU.mult, ALU.add
                        ).then_inc(sem["z_taken"], 1)
                if point == 7 and exists(k, 1):
                    dve.wait_ge(sem["rstd"], j + 1)
                    tsc(tiny[:, 3:4], tiny[:, 2:3], tiny[:, 1:2], None, ALU.mult).then_inc(sem["moments"], 1)
                    dve.wait_ge(sem["z_taken"], j + 1)
                    stt(z2[:], z1[:], tiny[:, 1:2], sums[:, 1, :], ALU.mult, ALU.add).then_inc(sem["z1"], 1)
                if point == 25 and exists(k, 1):
                    dve.wait_ge(sem["nrm"], j + 1)
                    dve.wait_ge(sem["z1"], j + 1)
                    since(dve, "zT_ready", j)
                    since(dve, "hin_ready", 2 * j)
                    nc.vector.tensor_copy(z[:, NS:3 * NS], z2[:, NS:3 * NS])
                    tsc(z[:, 0:NS], z2[:, 0:NS], tiny[:, 6:7], None, ALU.mult).then_inc(sem["zb"], 1)
                if point == LAST["dt", 0] + 1 and exists(k, 1):
                    dve.wait_ge(sem["dt_taken"], j + 1)
                    since(dve, "weighted", j)
                    tsc(ad[:], th[:], a01[:, 1:2], 1.0, ALU.mult, ALU.add).then_inc(sem["ad"], 1)
                    dve.wait_ge(sem["ad"], j + 1)
                    nc.vector.tensor_tensor_scan(pf[:, 1, 1:], ad[:, 1:], zeros[:, 1:], 1.0,
                                                 ALU.mult, ALU.add).then_inc(sem["scan_p"], 1)
                    dve.wait_ge(sem["scan_p"], j + 1)
                    nc.vector.reciprocal(pf[:, 0], pf[:, 1]).then_inc(sem["recip"], 1)
                    since(dve, "hend_taken", 2 * k)
                    nc.vector.tensor_copy(p_end[:, q:q + 1], pf[:, 1, P - 1:P])
                    nc.vector.tensor_copy(a0[:, q:q + 1], ad[:, 0:1])
                    dve.wait_ge(sem["recip"], j + 1)
                    since(dve, "y_ready", DB * k)
                    tt(bc[:, q, 0], zT[:, 0], pf[:, 0], ALU.mult)
                    tt(bc[:, q, 1].rearrange("n (r i) -> n i r", i=WAYS), zT[:, 1].rearrange("n (i r) -> n i r", r=NS),
                       pf[:, 1].rearrange("n (i r) -> n i r", r=NS), ALU.mult).then_inc(sem["weighted"], 1)
                    since(dve, "bound_out", 64 * j)
                    nc.vector.memset(bnd[:, :, 0:1], 0.0)
                    tsc(bnd[:, 0, 1:], pf[:, 0, 1:], -CLIP, None, ALU.mult)
                    tsc(bnd[:, 1, 1:], pf[:, 0, 1:], CLIP, None, ALU.mult).then_inc(sem["bound16"], 1)
                    dve.wait_ge(sem["bound16"], 2 * j + 1)
                    nc.vector.tensor_copy(bnd16[:, 0], bnd[:]).then_inc(sem["bound16"], 1)
                    dve.wait_ge(sem["bound16"], 2 * j + 2)
                    tt(bnd16[:, 1], bnd[:], bnd16[:, 0], ALU.subtract).then_inc(sem["bound_all"], 1)
                if point == LAST["mb", 0] and exists(k, 1):
                    dve.wait_ge(sem["mb_ready"], j + 1)
                    b = bank("mb")
                    since(dve, "tt_done", 2 * j)
                    tt(mT[:, q], b[:, 0:P], tri, ALU.mult)
                    tsc(nbh[:], b[:, P:P + NS], -1.0, None, ALU.mult).then_inc(sem["nb16"], 1)
                    nc.vector.tensor_copy(bq[:], b[:, P:P + NS]).then_inc(sem["nb16"], 1)
                    dve.wait_ge(sem["nb16"], 3 * j + 2)
                    stt(nbl[:], b[:, P:P + NS], -1.0, nbh[:], ALU.mult, ALU.subtract).then_inc(sem["nb16"], 1)
                    for d in range(2):
                        last = tt(bqm[:, q, :, d], bq[:].rearrange("s (o n) -> s o n", o=1).broadcast_to([P, NSUB + 1, NS]),
                                  prefix.rearrange("s (j o) -> s j o", o=1).broadcast_to([P, NSUB + 1, NS]), ALU.mult)
                    last.then_inc(sem["mb_taken"], 1)
                for i in range(2):
                    if point != LAST["hin", i] or not exists(k, 1):
                        continue
                    half = slice(i * BANK, (i + 1) * BANK)
                    dve.wait_ge(sem["hin_ready"], 2 * j + i + 1)
                    if isinstance(k, int) and j < BATCH:
                        nc.vector.tensor_copy(h1[:, q, half], bank("hin", i)[0:NS]).then_inc(sem["hin_taken"], 1)
                    else:
                        dve.wait_ge(sem["hend_taken"], 2 * (j - 2) + i + 1)
                        stt(h1[:, q, half], h1[:, q, half], a0[:, q:q + 1], bank("hin", i)[0:NS],
                            ALU.mult, ALU.add).then_inc(sem["hin_taken"], 1)
                    dve.wait_ge(sem["hin_taken"], 2 * j + i + 1)
                    tsc(h1[:, q, half], h1[:, q, half], CLIP, -CLIP, ALU.min, ALU.max).then_inc(sem["h1_done"], 1)
                for i in range(2):
                    if point != LAST["carry", i] + 1 or not exists(k, 1):
                        continue
                    half = slice(i * BANK, (i + 1) * BANK)
                    dve.wait_ge(sem["carry16"], 2 * j + i + 1)
                    dve.wait_ge(sem[f"xstack_in{q}"], N_XSTACK * pair(k, p, 1))
                    stt(cc[:, half], ch[:, half], neg_low, bank("carry", i), ALU.mult, ALU.add
                        ).then_inc(sem["carry_taken"], 1)
                if point == LAST["cr", 0] and exists(k, 0):
                    dve.wait_ge(sem["cr_ready"], k + 1)
                    since(dve, "y_ready", DB * k)
                    rep = bank("cr")[:, 0:P].rearrange("r (g e i) -> r g e i", g=4, e=4)
                    d = delta.rearrange("r (o i) -> r o i", o=1).broadcast_to([P, 4, WAYS])
                    for e in range(4):
                        last = tt(cst[:, :, e, WAYS * e:WAYS * (e + 1)], rep[:, :, e], d, ALU.mult)
                    last.then_inc(sem["cr_taken"], 1)
                for i in range(2):
                    if point != LAST["yT", i] + 1 or not exists(k, -1):
                        continue
                    dve.wait_ge(sem["yT_high"], 2 * (k - 1) + i + 1)
                    stt(yT[:, 1, 4 * i:4 * i + 4, :], bank("yT", i).rearrange("d (e t) -> d e t", e=4), 1.0,
                        yT[:, 0, 4 * i:4 * i + 4, :], ALU.mult, ALU.subtract).then_inc(sem["yT_taken"], 1)
                if point == LAST["out", 0] and exists(k, -1):
                    dve.wait_ge(sem["out_ready"], k)
                    dve.wait_ge(sem["res_in"], 16 * k)
                    stt(res[:], bank("out"), 1 / WS, res[:], ALU.mult, ALU.add).then_inc(sem["out_taken"], 1)

            def y_copy(k, p, u):
                dve.wait_ge(sem["y_ready"], DB * k + u + 1)
                if u % 4 == 0:
                    since(dve, "yT_ready", 2 * (k - 1) + u // 4 + 1)
                cut = slice(u * P, (u + 1) * P)
                nc.vector.tensor_copy(y[:, cut], bank("y", u)[:, 0:P]).then_inc(sem["y_taken"], 1)

            def ends(k, p, u):
                dve.wait_ge(sem["scanned"], TILES * k + NQ * (u + 1))
                since(dve, "hend_ready", 2 * (k - 1))
                nc.vector.tensor_copy(kend[:, p, u, :], ks[:, u % 2, :, P - 1]).then_inc(sem["kend_done"], 1)

            def body(k, p):
                def scan(s):
                    u, q = divmod(s, NQ)
                    g = TILES * k + s
                    dve.wait_ge(sem["lower_ready"], g + 1)
                    dve.wait_ge(sem["upper_copied"], g + 1)
                    if q == 0:
                        since(dve, "flipped", TILES * k + NQ * (u - 1))
                        since(dve, "kend_done", DB * k + u - 1)
                    nc.vector.tensor_tensor_scan(ks[:, u % 2, QN * q:QN * (q + 1)].rearrange("d n t -> d (n t)"),
                                                 ps_low[:, s % 2], upper[:, s % RING], 0.0,
                                                 ALU.max, ALU.min).then_inc(sem["scanned"], 1)

                for s in range(TILES):
                    if exists(k, 0) and s == 0:
                        scan(0)
                    if exists(k, 0) and s + 1 < TILES:
                        scan(s + 1)
                    if s == 0 and exists(k, -1):
                        ends(k - 1, 1 - p, DB - 1)
                    if s % NQ == 0 and s and exists(k, 0):
                        ends(k, p, s // NQ - 1)
                    for point in (2 * s, 2 * s + 1):
                        for _, _, name, i, off, _ in JOBS:
                            if name == "y" and LAST["y", i] == point and exists(k, off):
                                y_copy(k + off, (p + off) % 2, i)
                        side(k, p, point)

            steps(dve, body)

        @block.gpsimd
        def _(pool):
            tt, tsc = nc.gpsimd.tensor_tensor, nc.gpsimd.tensor_scalar
            pool.wait_ge(sem["const_in"], N_CONST)
            pool.wait_ge(sem["halo_set"], 2)
            pool.wait_ge(sem["prep"], 1)
            pool.wait_ge(sem["rowbc_taken"], 6)

            def body(k, p):
                j, q = k + 1, (p + 1) % 2
                for s in range(TILES):
                    if s == 1 and exists(k, 1):
                        pool.wait_ge(sem["norm_in"], j + 1)
                        since(pool, "z1", j)
                        tt(tiny[:, 1:2], tiny[:, 0:1], halfs[:, 0:1], ALU.pow).then_inc(sem["rstd"], 1)
                    if s == 7 and exists(k, 1):
                        pool.wait_ge(sem["xa"], j + 1)
                        tt(xn[:, q], xn[:, q], row_g[:], ALU.mult).then_inc(sem["xg"], 1)
                        pool.wait_ge(sem["xg"], j + 1)
                        tt(xn[:, q], xn[:, q], row_b[:], ALU.add).then_inc(sem["xn_done"], 1)
                    if s == 6 and exists(k, -1):
                        gated(k - 1, 1 - p, 1)
                    if s == 10 and exists(k, 1):
                        pool.wait_ge(sem["squares"], j + 1)
                        tt(tiny[:, 5:6], tiny[:, 4:5], halfs[:, 1:2], ALU.pow).then_inc(sem["root"], 1)
                        pool.wait_ge(sem["root"], j + 1)
                        carrier(p, 2 * TAPS)
                        tsc(tiny[:, 6:7], tiny[:, 5:6], 1.0, 0.0, ALU.min, ALU.max).then_inc(sem["nrm"], 1)
                        pool.wait_ge(sem["xh_done"], j + 1)
                        since(pool, f"stack_in{1 - q}", N_STACK * pair(k, p, 0))
                        tt(xl[:], xn[:, q], xh[:], ALU.subtract).then_inc(sem["xl_done"], 1)
                    if s == 13 and exists(k, 2):
                        pool.wait_ge(sem["xT_high"], k + 3)
                        tt(x16[:, 1], xf[:], x16[:, 0], ALU.subtract).then_inc(sem["xT_low"], 1)
                    if s == 27 and exists(k, 1):
                        pool.wait_ge(sem["xs_high"], k + 2)
                        tt(x16[:, 1], xf[:], x16[:, 0], ALU.subtract).then_inc(sem["xs_low"], 1)
                    if s in (2, 11) and exists(k, 0):
                        i = s // 11
                        half = slice(i * BANK, (i + 1) * BANK)
                        since(pool, "y_ready", DB * (k - 1) + 4 * (i + 1))
                        tt(dx[:, half], xn[:, p, half], row_d[:, half], ALU.mult).then_inc(sem["dx_done"], 1)
                    if s == 21 and exists(k, 1):
                        pool.wait_ge(sem["nb16"], 3 * (j + 1))
                        since(pool, f"stack_in{1 - q}", N_STACK * pair(k, p, 0))
                        m = submask.rearrange("s (o t) -> s o t", o=1).broadcast_to([P, NS, SUB])
                        for src, dst in ((nbh, tth), (nbl, ttl)):
                            tt(dst[:], src[:].rearrange("s (n o) -> s n o", o=1).broadcast_to([P, NS, SUB]), m,
                               ALU.mult).then_inc(sem["tt_done"], 1)
                    if 19 <= s < 27 and exists(k, 2):
                        convolve(k, p, *divmod(s - 19, TAPS))
                    if s == 24 and exists(k, 0):
                        gated(k, p, 0)

            def convolve(k, p, i, tap):
                n = 2 * (k + 2) + i
                part = slice(4 * i, 4 * i + 4)
                if tap == 0:
                    pool.wait_ge(sem["xr_taken"], n + 1)
                    since(pool, "silu_done", n - 1)
                if tap == 1:
                    since(pool, "xa", min(k + 2, STEPS) if isinstance(k, int) else k + 2)
                dst = tapped if tap else conv[:]
                if tap >= 2:
                    pool.wait_ge(sem["tap"], 3 * n + tap - 1)
                carrier(p, TAPS * i + tap)
                for d in range(4 * i, 4 * i + 4):
                    off = conv_b[:, p, d:d + 1] if tap == 0 else 0.0
                    last = tsc(dst[:, d, :], xr[:, p, d, tap:tap + P], cols[:, d, 3 + tap:4 + tap], off,
                               ALU.mult, ALU.add)
                last.then_inc(sem["tap_made"], 1)
                pool.wait_ge(sem["tap_made"], TAPS * n + tap + 1)
                if tap:
                    tt(conv[:, part], conv[:, part], tapped[:, part], ALU.add).then_inc(sem["tap"], 1)
                if tap == TAPS - 1:
                    nc.gpsimd.tensor_copy(xr[:, p, part, 0:TAPS - 1], xr[:, p, part, P:P + TAPS - 1]
                                          ).then_inc(sem["conv_done"], 1)

            def carrier(p, n):
                tt(idle[:, p, n:n + 1], halfs[:, 0:1], halfs[:, 1:2], ALU.mult)

            def gated(k, p, i):
                pool.wait_ge(sem["y_taken"], DB * k + 4 * (i + 1))
                pool.wait_ge(sem["gate_taken"], 2 * k + i + 1)
                half = slice(i * BANK, (i + 1) * BANK)
                tt(y[:, half], y[:, half], gate[:, half], ALU.mult).then_inc(sem["y_gated"], 1)

            steps(pool, body)


_OUT = "out_dram"


def kernel(x, cond_2048, L0_cond_W_in, L0_cond_W_conv, L0_cond_b_conv, L0_cond_ln_g, L0_cond_ln_b,
           L0_cond_W_xproj, L0_cond_W_dt, L0_cond_b_dt, L0_cond_A_log, L0_cond_D, L0_cond_W_out):
    import concourse.bacc as bacc
    from concourse.bass_utils import run_bass_kernel_spmd

    def col(v):
        return np.asarray(v).reshape(DB, P).T[:, :, None]

    taps = np.asarray(L0_cond_W_conv).reshape(DB, P, TAPS).transpose(1, 0, 2)
    cond = np.asarray(cond_2048).reshape(BATCH, DB, P).transpose(2, 1, 0)
    arrays = {
        "x": np.asarray(x).reshape(BATCH, SEQ // P, P, DM)[:, :, row_steps()].reshape(BATCH, SEQ, DM),
        "xT": np.asarray(x).transpose(0, 2, 1),
        "xTs": np.asarray(x).reshape(BATCH, SEQ // P, P, DM)[:, :, row_steps()].reshape(BATCH, SEQ, DM
                                                                                   ).transpose(0, 2, 1),
        "w_inT": np.asarray(L0_cond_W_in).T,
        "w_outT": np.asarray(L0_cond_W_out).T,
        "wxT": np.asarray(L0_cond_W_xproj).T,
        "cols": np.concatenate([col(L0_cond_ln_g), col(L0_cond_ln_b), col(L0_cond_b_conv), taps, cond], axis=2),
        "small": np.concatenate([np.asarray(L0_cond_W_dt).T, np.zeros((NS, 2 * NS), np.float32),
                                 np.asarray(L0_cond_b_dt)[:, None],
                                 np.asarray(L0_cond_A_log)[:, None]], axis=1),
        "rows": np.stack([np.asarray(v) for v in (L0_cond_ln_g, L0_cond_ln_b, L0_cond_D)]),
        **shape_constants(),
    }
    nc = bacc.Bacc("TRN2", target_bir_lowering=False, num_devices=1)
    ins, aps = {}, {}
    for name, a in arrays.items():
        a = np.ascontiguousarray(a)
        ins[f"in_{name}"] = a
        aps[name] = nc.dram_tensor(f"in_{name}", a.shape, mybir.dt.from_np(a.dtype), kind="ExternalInput").ap()
    out = nc.dram_tensor(_OUT, (BATCH, SEQ, DM), mybir.dt.float32, kind="ExternalOutput").ap()
    scratch = nc.dram_tensor("bounds_dram", (2, NSUB, 2, NS, SUB), mybir.dt.float16, kind="Internal").ap()
    build(nc, aps, out, scratch)
    r = run_bass_kernel_spmd(nc, [ins], core_ids=[0])
    rows = np.asarray(r.results[0][_OUT]).reshape(BATCH, SEQ // P, P, DM)
    return rows[:, :, np.argsort(row_steps())].reshape(BATCH, SEQ, DM)
```

```python
import numpy as np

import concourse.bass as bass
from concourse import mybir
from contextlib import ExitStack

BATCH, SEQ, DM, DI, NS, TAPS = 2, 2048, 512, 1024, 16, 4
P = 128
DB = DI // P
CB = DM // P
STEPS = BATCH * SEQ // P
SUB = 32
NSUB = P // SUB
NQ = 4
QN = NS // NQ
WAYS = P // NS
TILES = DB * NQ
BANK = 512
CLIP = 10.0
WS = 64.0
EPS = 1e-5
RING = 2
LAG = 4


def row_steps():
    return np.arange(P).reshape(WAYS, NS).T.reshape(-1)


def shape_constants():
    s = np.arange(P)
    t = np.arange(P)
    step = row_steps()
    tri = ((s[:, None] <= step[None, :]) & (s[:, None] >= 1)).astype(np.float32)
    shuffle = (t[:, None] == step[None, :]).astype(np.float32)
    r = np.arange(SUB)
    sub = ((r[:, None] <= r[None, :]) & (r[:, None] >= 1)).astype(np.float32)
    sub = np.tile(sub, (NSUB, 1))
    heads = np.array([P - 1] + [SUB * jj for jj in range(1, NSUB)])
    prefix = ((s[:, None] <= heads[None, :]) & (s[:, None] >= 1)).astype(np.float32)
    delta = np.tile(np.eye(WAYS, dtype=np.float32), (NS, 1))
    low = np.where((s % SUB) >= NS, -1.0, 0.0).astype(np.float32)[:, None]
    c128 = np.concatenate([np.eye(P, dtype=np.float32), tri, shuffle, sub, prefix, delta, low], axis=1)
    spread = np.repeat(np.eye(NS, dtype=np.float32), WAYS, axis=1)
    carry = np.zeros((2, NS, NSUB, 2, NS, SUB), np.float16)
    for n in range(NS):
        carry[:, n, 1:, :, n, :] = 1.0
        carry[:, n, 0, :, n, 0] = 1.0
    ones = np.ones((1, NSUB * DI), np.float16)
    return {"c128": c128, "spread": spread, "carry": carry.reshape(2 * NS, -1), "ones16": ones}


SEMS = """
xT_in xs_in xT_high xT_low xs_high xs_low w_piece0 w_piece1 w_piece2 w_piece3 w_high w_low res_in out_done0 out_done1 const_in fixed_in
xstack_in0 xstack_in1 stack_in0 stack_in1 bound_out bound_in0 bound_in1
gw_ready sums_ready sums_taken halo_set prep p16 act_prep
lower_ready upper_ready upper_copied scanned flipped flip_copied
xr_ready xr_taken xt_ready xt_taken z_ready z_taken zT_ready zT_taken dt_ready dt_taken
mb_ready mb_taken cr_ready cr_taken carry_ready carry_taken
hend_ready hend_taken y_ready y_taken yT_ready yT_taken gate_ready gate_taken
out_ready out_taken
conv_done tap0 tap silu_done stats aggr rstd moments z1 zb ad scan_p recip weighted bound16 bound_all
norm_in xa xg xn_done xh_done xl_done yT_high squares root nrm nb16 tt_done dx_done kend_done y_gated h1_done
carry16
row_out row_in h1_in0 h1_in1 h_scaled decay0 h1_high h1_low h1_raw
""".split()


def build(nc, A, out, scratch, row_dram):
    F, H = mybir.dt.float32, mybir.dt.float16
    ALU, ACT = mybir.AluOpType, mybir.ActivationFunctionType
    with ExitStack() as S:
        def sb(name, shape, dt=F):
            return S.enter_context(nc.sbuf_tensor(name, shape, dt))

        sem = {n: S.enter_context(nc.semaphore(n)) for n in SEMS}

        w_in = sb("w_in", [P, 2, CB, 2 * DI], H)
        w_out = sb("w_out", [P, 2, DB, DM], H)
        c128 = sb("c128_sb", [P, 3 * P + SUB + NSUB + WAYS + 1])
        at = 0
        parts = []
        for width in (P, P, P, SUB, NSUB, WAYS, 1):
            parts.append(c128[:, at:at + width])
            at += width
        ident, tri, shuffle, submask, prefix, delta, neg_low = parts
        spread = sb("spread_sb", [NS, P])
        cols = sb("cols_sb", [P, DB, 3 + TAPS + BATCH])
        small = sb("small_sb", [NS, 3 * NS + 2])
        row_g = sb("row_g", [P, DI])
        row_b = sb("row_b", [P, DI])
        row_d = sb("row_d", [P, DI])
        gw = sb("gw", [P, DB, 3 * NS])
        sums = sb("sums", [P, 2, 3 * NS])
        conv_b = sb("conv_b", [P, BATCH, DB])
        a01 = sb("a01", [NS, 2])
        halfs = sb("halfs", [P, 2])
        idle = sb("idle", [P, 2])
        zeros = sb("zeros", [NS, P])

        xf = sb("xf", [P, CB, P])
        x16 = sb("x16", [P, 2, CB, P], H)
        xr = sb("xr", [P, BATCH, DB, TAPS - 1 + P])
        conv = sb("conv", [P, DB, P])
        xcT = sb("xcT", [P, DB, P])
        yT = xcT[:].rearrange("d c t -> d (c t)").bitcast(H).rearrange("d (h c t) -> d h c t", h=2, c=DB)
        xc = sb("xc", [P, DI])
        wx = conv[:, :, 0:3 * NS]
        bw = conv[:, :, 3 * NS:6 * NS]
        ws = sb("ws", [P, 5, DB])
        xn = sb("xn", [P, 2, DI])
        xh = sb("xh", [P, DI], H)
        xl = sb("xl", [P, DI], H)
        st = sb("st", [P, 2, 6])
        mom = sb("mom", [P, 2])
        tiny = sb("tiny", [P, 8])

        z = sb("z", [P, 3 * NS])
        z1 = sb("z1", [P, 3 * NS])
        z2 = sb("z2", [P, 3 * NS])
        zT = sb("zT", [NS, 3, P])
        th = sb("th", [NS, P])
        ad = sb("ad", [NS, P])
        first_decay = sb("first_decay", [NS, 1])
        pf = sb("pf", [NS, 2, P])
        p_end = sb("p_end", [NS, 2])
        bc = sb("bc", [NS, 2, 2, P])
        bnd16 = sb("bnd16", [NS, 2, 2, P], H)
        mT = sb("mT", [P, 2, P])
        nbh = sb("nbh", [P, NS], H)
        nbl = sb("nbl", [P, NS], H)
        bqm = sb("bqm", [P, 2, NSUB, 2, NS], H)
        cst = sb("cst", [P, 4, 4, SUB])
        tth = sb("tth", [P, NS, SUB], H)
        ttl = sb("ttl", [P, NS, SUB], H)
        h1 = sb("h1", [NS, DI])
        lend = sb("lend", [NS, 2, DI])
        xn0 = conv[0:NS].rearrange("n c t -> n (c t)")
        h16 = xcT[0:NS].rearrange("n c t -> n (c t)").bitcast(H).rearrange("n (h d) -> n h d", h=2)
        ch = xh
        cc = xl

        xs = sb("xs", [P, 2, NSUB, DI], H)
        ts = sb("ts", [P, 2, NSUB, 2, NS * SUB], H)

        upper = sb("upper", [P, RING, BANK])
        ks = sb("ks", [P, 2, NS, P])
        kend = sb("kend", [P, 2, DB, NS])
        kT = sb("kT", [P, 2, 4, 4, P])

        gate = sb("gate", [P, DI])
        y = sb("y", [P, DI])
        ones = y[:, 0:P]
        dx = sb("dx", [P, BANK])
        res = sb("res", [P, DM])

        ps_low = S.enter_context(nc.psum_tensor("ps_low", [P, 2, BANK], F))
        ps_up = S.enter_context(nc.psum_tensor("ps_up", [P, 2, BANK], F))
        ps_flip = S.enter_context(nc.psum_tensor("ps_flip", [P, 2, BANK], F))
        ps_job = S.enter_context(nc.psum_tensor("ps_job", [P, 2, BANK], F))

        def since(eng, name, value):
            if isinstance(value, int) and value <= 0:
                return
            eng.wait_ge(sem[name], value)

        JOBS = [(0, 1, "z", 0, 1, 1), (2, 2, "y", 6, -1, 8), (4, 1, "yT", 0, -1, 2),
                (5, 4, "gate", 0, 0, 2), (10, 2, "y", 7, -1, 8), (12, 1, "hend", 0, -1, 2),
                (14, 1, "cr", 0, 0, 1), (15, 1, "hend", 1, -1, 2), (17, 1, "yT", 1, -1, 2),
                (18, 4, "gate", 1, 0, 2), (22, 2, "y", 0, 0, 8), (24, 5, "out", 0, -1, 1),
                (29, 1, "zT", 0, 1, 1), (30, 2, "y", 1, 0, 8), (32, 1, "dt", 0, 1, 1),
                (33, 4, "xr", 0, 2, 2), (37, 2, "y", 2, 0, 8), (39, 1, "mb", 0, 1, 1),
                (40, 4, "xr", 1, 2, 2), (44, 2, "y", 3, 0, 8), (47, 2, "carry", 0, 1, 2),
                (50, 2, "y", 4, 0, 8), (52, 2, "carry", 1, 1, 2), (56, 1, "xt", 0, 2, 2),
                (58, 2, "y", 5, 0, 8), (60, 1, "xt", 1, 2, 2)]
        assert len(JOBS) % 2 == 0
        LAST = {(name, i): first + parts - 1 for first, parts, name, i, _, _ in JOBS}
        CONV_AT = (LAST["xr", 0] + 1, LAST["xr", 1] + 1)
        SILU_AT = (46, 51)
        BANK_OF = {(name, i): m % 2 for m, (_, _, name, i, _, _) in enumerate(JOBS)}

        def exists(k, off):
            return not isinstance(k, int) or 0 <= k + off < STEPS

        def bank_free(pe, k, m):
            kk, mm = k, m
            while True:
                mm -= 2
                if mm < 0:
                    mm += len(JOBS)
                    kk = kk - 1
                    if isinstance(kk, int) and kk < -2:
                        return
                _, _, name, i, off, per = JOBS[mm]
                if exists(kk, off):
                    pe.wait_ge(sem[name + "_taken"], (kk + off) * per + i + 1)
                    return

        def steps(eng, body):
            for k in range(-2, 2):
                body(k, k % 2)
            with eng.Fori(2, STEPS - 2, 2) as k0:
                body(k0, 0)
                body(k0 + 1, 1)
            for k in range(STEPS - 2, STEPS + 1):
                body(k, k % 2)

        staged = [ks[:, h].rearrange("p n t -> p (n t)") for h in range(2)]
        staged += [kT[:, h].rearrange("p g e d -> p (g e d)") for h in range(2)]
        STAGED = len(staged)
        w_in_dram = A["w_inT"].rearrange("(c p) d -> p c d", p=P)
        w_out_dram = A["w_outT"].rearrange("(h c p) d -> p h c d", p=P, h=2)
        pieces = [(w_in_dram[:, c], w_in[:, 0, c], w_in[:, 1, c]) for c in range(CB)]
        for g in range(2):
            part = slice(g * DB // 2, (g + 1) * DB // 2)
            pieces.append((w_out_dram[:, g], w_out[:, 0, part], w_out[:, 1, part]))

        def staged_like(n, piece):
            flat = staged[n % STAGED]
            return flat if len(piece.shape) == 2 else flat.rearrange("p (c d) -> p c d", d=piece.shape[2])

        block = S.enter_context(nc.Block())

        @block.sync
        def _(sp):
            for dst, src in ((c128[:], A["c128"]), (cols[:], A["cols"]),
                             (wx, A["wxT"].rearrange("(c p) m -> p c m", p=P)), (small[:], A["small"])):
                sp.dma_start(dst, src).then_inc(sem["const_in"], 16)

            def load_piece(n):
                src = pieces[n][0]
                sp.dma_start(staged_like(n, src), src).then_inc(sem[f"w_piece{n % STAGED}"], 16)

            for n in range(STAGED):
                load_piece(n)
            loads = [(spread[:], A["spread"])]
            for i, row in enumerate((row_g, row_b, row_d)):
                loads.append((row[:], A["rows"][i:i + 1].broadcast_to([P, DI])))
            for p in range(2):
                carry = A["carry"].rearrange("r (j c) -> r j c", j=NSUB)
                loads.append((ts[96:128, p].rearrange("r j v c -> r j (v c)"), carry))
                for r in (0, 32):
                    loads.append((xs[r:r + 1, p], A["ones16"].rearrange("o (j d) -> o j d", j=NSUB)))
            for dst, src in loads:
                sp.dma_start(dst, src).then_inc(sem["fixed_in"], 16)
            for n in range(STAGED, len(pieces)):
                sp.wait_ge(sem["w_high"], n - STAGED + 1)
                sp.wait_ge(sem["w_low"], n - STAGED + 1)
                load_piece(n)

            xT_dram = A["xT"].rearrange("b (c p) t -> b p c t", p=P)
            xTs_dram = A["xTs"].rearrange("b (c p) t -> b p c t", p=P)
            x_dram = A["x"]

            def body(k, p):
                def chunk(off):
                    b = (p + off) % 2
                    c = (k + off - b) // 2 if isinstance(k, int) else (k + (off - b)) // 2
                    return b, c

                if exists(k, 2):
                    b, c = chunk(2)
                    before = ("xs_high", "xs_low")
                    if isinstance(k, int) and k == -1:
                        before = ("xT_high", "xT_low")
                    for name in before:
                        since(sp, name, max(k + 1, 1) if isinstance(k, int) and k == -1 else k + 1)
                    sp.dma_start(xf[:], xT_dram[b, :, :, bass.ds(c * P, P)]).then_inc(sem["xT_in"], 16)
                if exists(k, -1):
                    b, c = chunk(-1)
                    if not (isinstance(k, int) and k < 2):
                        sp.wait_ge(sem[f"out_done{p}"], 16 * ((k - p) // 2))
                    sp.dma_start(res[:], x_dram[b, bass.ds(c * P, P), :]).then_inc(sem["res_in"], 16)
                if exists(k, 1):
                    j, pn = k + 1, (p + 1) % 2
                    xstack, stack = sem[f"xstack_in{pn}"], sem[f"stack_in{pn}"]
                    since(sp, "upper_ready", TILES * k)
                    sp.wait_ge(sem["xn_done"], j + 1)
                    sp.dma_start(row_dram, xn[0:1, pn]).then_inc(sem["row_out"], 16)
                    sp.wait_ge(sem["xh_done"], j + 1)
                    for jj in range(NSUB):
                        a = SUB * jj
                        sp.dma_start(xs[1:SUB, pn, jj], xh[a + 1:a + SUB]).then_inc(xstack, 16)
                        sp.dma_start(xs[SUB + 1:2 * SUB, pn, jj], xh[a + 1:a + SUB]).then_inc(xstack, 16)
                    sp.wait_ge(sem["xl_done"], j + 1)
                    for jj in range(NSUB):
                        a = SUB * jj
                        sp.dma_start(xs[2 * SUB:3 * SUB, pn, jj], xl[a:a + SUB]).then_inc(xstack, 16)
                    sp.wait_ge(sem["row_out"], 16 * (j + 1))
                    sp.dma_start(xn0, row_dram.broadcast_to([NS, DI])).then_inc(sem["row_in"], 16)
                    b, c = chunk(1)
                    if exists(k, 2):
                        sp.wait_ge(sem["xT_high"], k + 3)
                        sp.wait_ge(sem["xT_low"], k + 3)
                    else:
                        sp.wait_ge(sem["xs_low"], k + 1)
                        sp.wait_ge(sem["xs_high"], k + 1)
                    sp.dma_start(xf[:], xTs_dram[b, :, :, bass.ds(c * P, P)]).then_inc(sem["xs_in"], 16)
                if exists(k, -1):
                    b, c = chunk(-1)
                    sp.wait_ge(sem["out_taken"], k)
                    sp.dma_start(out[b, bass.ds(c * P, P), :], res[:]).then_inc(sem[f"out_done{b}"], 16)
                if exists(k, 1):
                    sp.wait_ge(sem["bound_all"], 2 * (j + 1))
                    for h in range(2):
                        for v in range(2):
                            sp.dma_start(scratch[h, :, v].rearrange("j n t -> n j t"),
                                         bnd16[:, h, v].rearrange("n (j t) -> n j t", j=NSUB)
                                         ).then_inc(sem["bound_out"], 16)
                    sp.wait_ge(sem["bound_out"], 64 * (j + 1))
                    for h in range(2):
                        sp.dma_start(ts[SUB * h:SUB * h + 1, pn].rearrange("o j v c -> o (j v c)"),
                                     scratch[h].rearrange("(o j) v n t -> o (j v n t)", o=1)
                                     ).then_inc(sem[f"bound_in{pn}"], 16)
                    sp.wait_ge(sem["h1_low"], j + 1)
                    for h in range(2):
                        row = 3 * SUB + NS * h
                        sp.dma_start(xs[row:row + NS, pn, 0], h16[:, h]).then_inc(sem[f"h1_in{pn}"], 16)
                    sp.wait_ge(sem["tt_done"], 2 * (j + 1))
                    for jj in range(NSUB):
                        a = SUB * jj
                        for r, half in ((0, tth), (SUB, ttl), (2 * SUB, tth)):
                            lead = 0 if r == 2 * SUB else 1
                            rows = half[a + lead:a + SUB].rearrange("s (o n) t -> s o (n t)", o=1)
                            sp.dma_start(ts[r + lead:r + SUB, pn, jj],
                                         rows.broadcast_to([SUB - lead, 2, NS * SUB])).then_inc(stack, 16)
                    sp.wait_ge(sem["carry_taken"], 2 * j + 2)
                    for jj in range(1, NSUB):
                        sp.dma_start(xs[3 * SUB:P, pn, jj], cc[SUB * jj:SUB * jj + SUB]).then_inc(stack, 16)

            steps(sp, body)
            for b in range(BATCH):
                sp.wait_ge(sem[f"out_done{b}"], 16 * (STEPS // BATCH))
            sp.wait_ge(sem["bound_out"], 64 * STEPS)
            sp.wait_ge(sem["row_out"], 16 * STEPS)

        N_CONST = 16 * 4
        N_FIXED = 16 * 10
        N_XSTACK = 16 * 3 * NSUB
        N_STACK = 16 * (3 * NSUB + NSUB - 1)
        N_BOUND = 16 * 2
        N_H1 = 16 * 2

        def first_chunk(j):
            return isinstance(j, int) and j < BATCH

        def pair(k, p, off):
            q = (p + off) % 2
            return (k + off - q) // 2 + 1

        @block.tensor
        def _(pe):
            mm = nc.tensor.matmul
            tr = nc.tensor.transpose
            pe.wait_ge(sem["const_in"], N_CONST)
            pe.wait_ge(sem["prep"], 1)
            pe.wait_ge(sem["gw_ready"], 2)
            for i, src in enumerate((gw, bw)):
                for c in range(DB):
                    last = mm(ps_up[:, i, 0:3 * NS], ones, src[:, c], start=(c == 0), stop=(c == DB - 1))
                last.then_inc(sem["sums_ready"], 1)
            pe.wait_ge(sem["sums_taken"], 1)
            pe.wait_ge(sem["fixed_in"], N_FIXED)
            pe.wait_ge(sem["w_low"], len(pieces))
            pe.wait_ge(sem["w_high"], len(pieces))
            PASSES = ((0, 0), (0, 1), (1, 0))

            def job(k, p, m, part):
                _, parts, name, i, off, per = JOBS[m]
                if not exists(k, off):
                    return
                j = k + off
                q = (p + off) % 2
                ps = ps_job[:, m % 2]
                ready = sem[name + "_ready"]
                half = slice(i * BANK, (i + 1) * BANK)
                if part == 0:
                    inputs(j, q, name, i)
                    bank_free(pe, k, m)

                def share(n):
                    return range(part * n // parts, (part + 1) * n // parts)

                if name == "xr":
                    for e in share(4):
                        d = (4 * i + e) * P
                        for c in range(CB):
                            for n, (a, b) in enumerate(PASSES):
                                last = mm(ps[:, e * P:(e + 1) * P], w_in[:, a, c, d:d + P], x16[:, b, c, :],
                                          start=(c == n == 0), stop=(c == CB - 1 and n == 2))
                elif name == "gate":
                    for c in share(CB):
                        for n, (a, b) in enumerate(PASSES):
                            last = mm(ps, x16[:, a, c, :], w_in[:, b, c, DI + i * BANK:DI + (i + 1) * BANK],
                                      start=(c == n == 0), stop=(c == CB - 1 and n == 2))
                elif name == "xt":
                    for e in range(4):
                        last = tr(ps[:, e * P:(e + 1) * P], xcT[:, 4 * i + e, :], ident)
                elif name == "z":
                    for c in range(DB):
                        last = mm(ps[:, 0:3 * NS], xcT[:, c, :], gw[:, c, :], start=(c == 0), stop=(c == DB - 1))
                elif name == "zT":
                    for e in range(3):
                        last = tr(ps[0:NS, e * P:(e + 1) * P], z[:, e * NS:(e + 1) * NS], ident)
                elif name == "dt":
                    last = mm(ps[0:3 * NS, 0:P], small[:, 0:3 * NS], zT[:, 2, :], start=True, stop=True)
                elif name == "mb":
                    mm(ps[:, 0:P], bc[:, q, 0, :], bc[:, q, 1, :], start=True, stop=True)
                    last = tr(ps[:, P:P + NS], bc[:, q, 0, :], ident[0:NS, 0:NS])
                elif name == "cr":
                    last = mm(ps[:, 0:P], spread[:], bc[:, q, 1, :], start=True, stop=True)
                elif name == "carry":
                    for a, b in (((0, 0),), ((0, 1), (1, 0)))[part]:
                        last = mm(ps, bqm[:, a].rearrange("s j d n -> s (j d n)"), (xh, xl)[b][:, half],
                                  start=(a == b == 0), stop=(a == 1))
                elif name == "hend":
                    for e in range(4):
                        last = tr(ps[0:NS, e * P:(e + 1) * P], kend[:, q, 4 * i + e, :], ident)
                elif name == "y":
                    if part == 0:
                        mm(ps[:, 0:P], mT[:, q, :], xn[:, q, i * P:(i + 1) * P], start=True, stop=False)
                        mm(ps[:, 0:P], shuffle, dx[:, i % 4 * P:(i % 4 + 1) * P], start=False, stop=False)
                    for e in share(4):
                        for g in range(4):
                            last = mm(ps[SUB * g:SUB * (g + 1), 0:P], cst[:, g, e, :], kT[:, i % 2, g, e, :],
                                      start=False, stop=(e == 3))
                elif name == "yT":
                    for e in range(4):
                        d = 4 * i + e
                        last = tr(ps[:, e * P:(e + 1) * P], y[:, d * P:(d + 1) * P], ident)
                elif name == "out":
                    for c in share(DB):
                        for n, (a, b) in enumerate(PASSES):
                            last = mm(ps, yT[:, a, c, :], w_out[:, b, c, :], start=(c == n == 0),
                                      stop=(c == DB - 1 and n == 2))
                if part == parts - 1:
                    last.then_inc(ready, 1)

            def inputs(j, q, name, i):
                if name == "xr":
                    pe.wait_ge(sem["xT_high"], j + 1)
                    pe.wait_ge(sem["xT_low"], j + 1)
                elif name == "gate":
                    pe.wait_ge(sem["xs_high"], j + 1)
                    pe.wait_ge(sem["xs_low"], j + 1)
                elif name == "xt":
                    pe.wait_ge(sem["silu_done"], 2 * j + i + 1)
                elif name == "z":
                    pe.wait_ge(sem["silu_done"], 2 * (j + 1))
                elif name == "zT":
                    pe.wait_ge(sem["zb"], j + 1)
                elif name == "dt":
                    pe.wait_ge(sem["zT_taken"], j + 1)
                elif name in ("mb", "cr"):
                    pe.wait_ge(sem["weighted"], j + 1)
                elif name == "carry":
                    pe.wait_ge(sem["mb_taken"], j + 1)
                    pe.wait_ge(sem["xh_done"], j + 1)
                    pe.wait_ge(sem["xl_done"], j + 1)
                elif name == "hend":
                    pe.wait_ge(sem["kend_done"], DB * (j + 1))
                elif name == "y":
                    pe.wait_ge(sem["flip_copied"], TILES * j + NQ * (i + 1))
                    if i == 0:
                        pe.wait_ge(sem["cr_taken"], j + 1)
                    if i % 4 == 0:
                        pe.wait_ge(sem["dx_done"], 2 * j + i // 4 + 1)
                elif name == "yT":
                    pe.wait_ge(sem["y_gated"], 2 * j + i + 1)
                elif name == "out":
                    pe.wait_ge(sem["yT_taken"], 2 * (j + 1))

            def fill(k, p, s):
                g = TILES * k + s
                u, q = divmod(s, NQ)
                if s == 0:
                    pe.wait_ge(sem[f"xstack_in{p}"], N_XSTACK * pair(k, p, 0))
                    pe.wait_ge(sem[f"stack_in{p}"], N_STACK * pair(k, p, 0))
                    pe.wait_ge(sem[f"bound_in{p}"], N_BOUND * pair(k, p, 0))
                    pe.wait_ge(sem[f"h1_in{p}"], N_H1 * pair(k, p, 0))
                for v, ps, free, ready in ((1, ps_up, "upper_copied", "upper_ready"),
                                           (0, ps_low, "scanned", "lower_ready")):
                    since(pe, free, g - 1)
                    o = ps[:, s % 2].rearrange("d (n t) -> d n t", n=QN)
                    for jj in range(NSUB):
                        last = mm(o[:, :, SUB * jj:SUB * (jj + 1)], xs[:, p, jj, u * P:(u + 1) * P],
                                  ts[:, p, jj, v, q * QN * SUB:(q + 1) * QN * SUB].rearrange("s (n t) -> s n t", n=QN),
                                  start=True, stop=True)
                    last.then_inc(sem[ready], 1)

            def flip(k, p, s):
                g = TILES * k + s
                u, q = divmod(s, NQ)
                if q == 0:
                    pe.wait_ge(sem["scanned"], g + NQ)
                since(pe, "flip_copied", g - 1)
                flat = ks[:, u % 2].rearrange("d n t -> d (n t)")
                for e in range(4):
                    last = tr(ps_flip[:, s % 2, e * P:(e + 1) * P], flat[:, bass.ds(4 * q + e, P, step=NS)], ident)
                last.then_inc(sem["flipped"], 1)

            def jobs_at(k, p, point):
                for m, (first, parts, *_) in enumerate(JOBS):
                    if first <= point < first + parts:
                        job(k, p, m, point - first)

            def body(k, p):
                for s in range(TILES):
                    if exists(k, 0) and s == 0:
                        fill(k, p, 0)
                    if exists(k, 0) and s + 1 < TILES:
                        fill(k, p, s + 1)
                    jobs_at(k, p, 2 * s)
                    t = s - LAG
                    if t >= 0 and exists(k, 0):
                        flip(k, p, t)
                    elif t < 0 and exists(k, -1):
                        flip(k - 1, 1 - p, t + TILES)
                    jobs_at(k, p, 2 * s + 1)

            steps(pe, body)

        @block.scalar
        def _(act):
            copy, act_fn = nc.scalar.copy, nc.scalar.activation
            act.wait_ge(sem["const_in"], N_CONST)
            act.wait_ge(sem["halo_set"], 2)
            act_fn(tiny[:, 7:8], cols[:, 0, 0:1], ACT.Silu).then_inc(sem["act_prep"], 1)
            act_fn(a01[:, 0:1], small[:, 3 * NS + 1:3 * NS + 2], ACT.Tanh).then_inc(sem["act_prep"], 1)
            for n, (_, high, _) in enumerate(pieces):
                act.wait_ge(sem[f"w_piece{n % STAGED}"], 16 * (n // STAGED + 1))
                act_fn(high, staged_like(n, high), ACT.Identity, scale=WS).then_inc(sem["w_high"], 1)
                if n == 1:
                    act.wait_ge(sem["sums_ready"], 2)
                    copy(sums[:], ps_up[:, :, 0:3 * NS]).then_inc(sem["sums_taken"], 1)

            def bank(name, i=0):
                return ps_job[:, BANK_OF[name, i]]

            def side(k, p, point):
                def take(name, i, off, per):
                    act.wait_ge(sem[name + "_ready"], (k + off) * per + i + 1)

                def at(name, off, per=2):
                    return [i for i in range(per) if LAST[name, i] == point and exists(k, off)]

                if point == 16 and exists(k, 1):
                    j, q = k + 1, (p + 1) % 2
                    act.wait_ge(sem["moments"], j + 1)
                    act.wait_ge(sem["xt_taken"], 2 * (j + 1))
                    since(act, "y_ready", DB * k)
                    since(act, "row_out", 16 * k)
                    act_fn(xn[:, q], xc[:], ACT.Identity, scale=tiny[:, 1:2],
                           bias=tiny[:, 3:4]).then_inc(sem["xa"], 1)
                for i in at("yT", -1):
                    take("yT", i, -1, 2)
                    since(act, "z_ready", min(k + 2, STEPS) if isinstance(k, int) else k + 2)
                    copy(yT[:, 0, 4 * i:4 * i + 4, :],
                         bank("yT", i).rearrange("d (e t) -> d e t", e=4)).then_inc(sem["yT_high"], 1)
                for i in at("gate", 0):
                    take("gate", i, 0, 2)
                    since(act, "y_gated", 2 * (k - 1) + i + 1)
                    act_fn(gate[:, i * BANK:(i + 1) * BANK], bank("gate", i), ACT.Silu, scale=1 / WS
                           ).then_inc(sem["gate_taken"], 1)
                if point == 23 and exists(k, 1):
                    j, q = k + 1, (p + 1) % 2
                    act.wait_ge(sem["xn_done"], j + 1)
                    since(act, "carry_taken", 2 * j)
                    act_fn(ch[:], xn[:, q], ACT.Square, accum_out=tiny[:, 4:5]).then_inc(sem["squares"], 1)
                    act.wait_ge(sem["squares"], j + 1)
                    act_fn(xh[:], xn[:, q], ACT.Identity).then_inc(sem["xh_done"], 1)
                if point == 25 and exists(k, 2):
                    act.wait_ge(sem["xT_in"], 16 * (k + 3))
                    since(act, "gate_ready", 2 * (k + 1))
                    if isinstance(k, int) and k == -1:
                        act.wait_ge(sem["xr_ready"], 2)
                    copy(x16[:, 0], xf[:]).then_inc(sem["xT_high"], 1)
                for _ in at("zT", 1, 1):
                    take("zT", 0, 1, 1)
                    since(act, "h1_raw", k + 1)
                    copy(zT[:], bank("zT")[0:NS, 0:3 * P].rearrange("n (e t) -> n e t", e=3)
                         ).then_inc(sem["zT_taken"], 1)
                for _ in at("dt", 1, 1):
                    take("dt", 0, 1, 1)
                    act_fn(th[:], bank("dt")[0:NS, 0:P], ACT.Tanh, bias=small[:, 3 * NS:3 * NS + 1]
                           ).then_inc(sem["dt_taken"], 1)
                if point in (LAST["xr", 0] + 1, LAST["xr", 1] + 1) and exists(k, 2):
                    i = int(point > LAST["xr", 1])
                    act.wait_ge(sem["xr_taken"], 2 * (k + 2) + i + 1)
                    since(act, "silu_done", 2 * (k + 1) + i + 1)
                    if exists(k, 1):
                        act.wait_ge(sem["h1_raw"], k + 2)
                    for d in range(4 * i, 4 * i + 4):
                        last = act_fn(conv[:, d, :], xr[:, p, d, 0:P], ACT.Identity, scale=cols[:, d, 3:4],
                                      bias=conv_b[:, p, d:d + 1])
                    last.then_inc(sem["tap0"], 1)
                if point == 34 and exists(k, 1) and not first_chunk(k + 1):
                    act.wait_ge(sem["hend_taken"], 2 * k)
                    act.wait_ge(sem["decay0"], k + 2)
                    act_fn(h1[:], h1[:], ACT.Identity, scale=first_decay[:]).then_inc(sem["h_scaled"], 1)
                if point == 38 and exists(k, 1):
                    act.wait_ge(sem["h1_done"], k + 2)
                    since(act, "out_ready", k)
                    copy(h16[:, 0], h1[:]).then_inc(sem["h1_high"], 1)
                for i in at("xr", 2):
                    take("xr", i, 2, 2)
                    since(act, "conv_done", 2 * (k + 1) + i + 1)
                    act_fn(xr[:, p, 4 * i:4 * i + 4, TAPS - 1:], bank("xr", i).rearrange("d (e t) -> d e t", e=4),
                           ACT.Identity, scale=1 / WS).then_inc(sem["xr_taken"], 1)
                if point == 46 and exists(k, 1):
                    act.wait_ge(sem["xs_in"], 16 * (k + 2))
                    since(act, "xr_ready", min(2 * (k + 3), 2 * STEPS) if isinstance(k, int) else 2 * (k + 3))
                    since(act, "gate_ready", 2 * (k + 1))
                    copy(x16[:, 0], xf[:]).then_inc(sem["xs_high"], 1)
                if point in SILU_AT and exists(k, 2):
                    i = SILU_AT.index(point)
                    part = slice(4 * i, 4 * i + 4)
                    act.wait_ge(sem["tap"], (TAPS - 1) * (2 * (k + 2) + i + 1))
                    since(act, "z_ready", min(k + 2, STEPS) if isinstance(k, int) else k + 2)
                    since(act, "out_ready", k)
                    if exists(k, 1):
                        act.wait_ge(sem[f"h1_in{1 - p}"], N_H1 * pair(k, p, 1))
                    act_fn(xcT[:, part], conv[:, part], ACT.Silu).then_inc(sem["silu_done"], 1)
                for i in at("xt", 2):
                    take("xt", i, 2, 2)
                    since(act, "xa", k + 2)
                    copy(xc[:, i * BANK:(i + 1) * BANK], bank("xt", i)).then_inc(sem["xt_taken"], 1)
                for i in at("carry", 1):
                    take("carry", i, 1, 2)
                    act.wait_ge(sem[f"xstack_in{1 - p}"], N_XSTACK * pair(k, p, 1))
                    copy(ch[:, i * BANK:(i + 1) * BANK], bank("carry", i)).then_inc(sem["carry16"], 1)

            def copy_flip(k, p, s):
                g = TILES * k + s
                u, q = divmod(s, NQ)
                act.wait_ge(sem["flipped"], g + 1)
                since(act, "y_ready", DB * k + u - 1)
                copy(kT[:, u % 2, q], ps_flip[:, s % 2].rearrange("r (e d) -> r e d", e=4)
                     ).then_inc(sem["flip_copied"], 1)

            def body(k, p):
                def copy_upper(s):
                    g = TILES * k + s
                    act.wait_ge(sem["upper_ready"], g + 1)
                    since(act, "scanned", g - RING + 1)
                    copy(upper[:, s % RING], ps_up[:, s % 2]).then_inc(sem["upper_copied"], 1)

                for s in range(TILES):
                    if exists(k, 0) and s == 0:
                        copy_upper(0)
                    if exists(k, 0) and s + 1 < TILES:
                        copy_upper(s + 1)
                    side(k, p, 2 * s)
                    t = s - LAG
                    if t >= 0 and exists(k, 0):
                        copy_flip(k, p, t)
                    elif t < 0 and exists(k, -1):
                        copy_flip(k - 1, 1 - p, t + TILES)
                    side(k, p, 2 * s + 1)

            steps(act, body)

        @block.vector
        def _(dve):
            tt, tsc, stt = nc.vector.tensor_tensor, nc.vector.tensor_scalar, nc.vector.scalar_tensor_tensor
            nc.vector.memset(ones, 1.0)
            nc.vector.memset(zeros[:], 0.0)
            nc.vector.memset(halfs[:, 0:1], -0.5)
            nc.vector.memset(halfs[:, 1:2], 0.5)
            nc.vector.memset(pf[:, 1, 0:1], 1.0)
            nc.vector.memset(bnd16[:, :, :, 0:1], 0.0)
            nc.vector.memset(p_end[:], 1.0)
            nc.vector.memset(cst[:], 0.0).then_inc(sem["prep"], 1)
            dve.wait_ge(sem["const_in"], N_CONST)
            tt(gw[:], wx, cols[:, :, 0:1].broadcast_to([P, DB, 3 * NS]), ALU.mult).then_inc(sem["gw_ready"], 1)
            tt(bw, wx, cols[:, :, 1:2].broadcast_to([P, DB, 3 * NS]), ALU.mult).then_inc(sem["gw_ready"], 1)
            tap0 = 3
            tt(ws[:, 0, :], cols[:, :, tap0], cols[:, :, tap0 + 1], ALU.add).then_inc(sem["p16"], 1)
            tt(ws[:, 1, :], cols[:, :, tap0 + 2], cols[:, :, tap0 + 3], ALU.add).then_inc(sem["p16"], 1)
            dve.wait_ge(sem["p16"], 2)
            tt(ws[:, 2, :], ws[:, 0, :], ws[:, 1, :], ALU.add).then_inc(sem["p16"], 1)
            dve.wait_ge(sem["p16"], 3)
            for b in range(BATCH):
                cond = cols[:, :, 3 + TAPS + b]
                tt(ws[:, 3 + b, :], ws[:, 2, :], cond, ALU.mult).then_inc(sem["p16"], 1)
                dve.wait_ge(sem["p16"], 4 + b)
                tt(conv_b[:, b, :], ws[:, 3 + b, :], cols[:, :, 2], ALU.add)
                tsc(xr[:, b, :, 0:TAPS - 1],
                    cols[:, :, 3 + TAPS + b:4 + TAPS + b].broadcast_to([P, DB, TAPS - 1]),
                    -1.0, None, ALU.mult).then_inc(sem["halo_set"], 1)
            dve.wait_ge(sem["act_prep"], 2)
            tsc(a01[:, 1:2], a01[:, 0:1], -0.01, None, ALU.mult).then_inc(sem["p16"], 1)
            dve.wait_ge(sem["p16"], 6)
            for n, (_, high, low) in enumerate(pieces):
                dve.wait_ge(sem["w_high"], n + 1)
                stt(low, staged_like(n, low), WS, high, ALU.mult, ALU.subtract).then_inc(sem["w_low"], 1)

            def bank(name, i=0):
                return ps_job[:, BANK_OF[name, i]]

            def side(k, p, point):
                j, q = k + 1, (p + 1) % 2
                if point == 0 and exists(k, 1):
                    dve.wait_ge(sem["xt_taken"], 2 * (j + 1))
                    nc.vector.bn_stats(st[:, 0], xc[:, 0:BANK]).then_inc(sem["stats"], 1)
                    nc.vector.bn_stats(st[:, 1], xc[:, BANK:]).then_inc(sem["stats"], 1)
                    dve.wait_ge(sem["stats"], 2 * (j + 1))
                    since(dve, "xa", j)
                    nc.vector.memset(tiny[:, 7:8], 0.0)
                    nc.vector.bn_aggr(mom[:], st[:].rearrange("p a b -> p (a b)")).then_inc(sem["aggr"], 1)
                    dve.wait_ge(sem["aggr"], j + 1)
                    tsc(tiny[:, 0:1], mom[:, 1:2], EPS, None, ALU.add)
                    tsc(tiny[:, 2:3], mom[:, 0:1], -1.0, None, ALU.mult).then_inc(sem["norm_in"], 1)
                if point == 2 and exists(k, 1):
                    dve.wait_ge(sem["norm_in"], j + 1)
                    dve.wait_ge(sem["z_ready"], j + 1)
                    stt(z1[:], sums[:, 0, :], tiny[:, 2:3], bank("z")[:, 0:3 * NS], ALU.mult, ALU.add
                        ).then_inc(sem["z_taken"], 1)
                if point == 7 and exists(k, 1):
                    dve.wait_ge(sem["rstd"], j + 1)
                    tsc(tiny[:, 3:4], tiny[:, 2:3], tiny[:, 1:2], None, ALU.mult).then_inc(sem["moments"], 1)
                    dve.wait_ge(sem["z_taken"], j + 1)
                    stt(z2[:], z1[:], tiny[:, 1:2], sums[:, 1, :], ALU.mult, ALU.add).then_inc(sem["z1"], 1)
                if point == 25 and exists(k, 1):
                    dve.wait_ge(sem["nrm"], j + 1)
                    dve.wait_ge(sem["z1"], j + 1)
                    since(dve, "zT_ready", j)
                    nc.vector.tensor_copy(z[:, NS:3 * NS], z2[:, NS:3 * NS])
                    tsc(z[:, 0:NS], z2[:, 0:NS], tiny[:, 6:7], None, ALU.mult).then_inc(sem["zb"], 1)
                if point == LAST["dt", 0] + 1 and exists(k, 1):
                    dve.wait_ge(sem["dt_taken"], j + 1)
                    since(dve, "weighted", j)
                    tsc(ad[:], th[:], a01[:, 1:2], 1.0, ALU.mult, ALU.add).then_inc(sem["ad"], 1)
                    dve.wait_ge(sem["ad"], j + 1)
                    nc.vector.tensor_tensor_scan(pf[:, 1, 1:], ad[:, 1:], zeros[:, 1:], 1.0,
                                                 ALU.mult, ALU.add).then_inc(sem["scan_p"], 1)
                    dve.wait_ge(sem["scan_p"], j + 1)
                    nc.vector.reciprocal(pf[:, 0], pf[:, 1]).then_inc(sem["recip"], 1)
                    if not first_chunk(j):
                        since(dve, "h_scaled", k - 1)
                    tt(first_decay[:], ad[:, 0:1], p_end[:, q:q + 1], ALU.mult).then_inc(sem["decay0"], 1)
                    dve.wait_ge(sem["recip"], j + 1)
                    dve.wait_ge(sem["decay0"], j + 1)
                    nc.vector.tensor_copy(p_end[:, q:q + 1], pf[:, 1, P - 1:P])
                    since(dve, "y_ready", DB * k)
                    tt(bc[:, q, 0], zT[:, 0], pf[:, 0], ALU.mult)
                    tt(bc[:, q, 1].rearrange("n (r i) -> n i r", i=WAYS), zT[:, 1].rearrange("n (i r) -> n i r", r=NS),
                       pf[:, 1].rearrange("n (i r) -> n i r", r=NS), ALU.mult).then_inc(sem["weighted"], 1)
                    since(dve, "bound_out", 64 * j)
                    for v, clip in enumerate((-CLIP, CLIP)):
                        tsc(bnd16[:, 0, v, 1:], pf[:, 0, 1:], clip, None, ALU.mult).then_inc(sem["bound16"], 1)
                    for v, clip in enumerate((-CLIP, CLIP)):
                        dve.wait_ge(sem["bound16"], 2 * j + v + 1)
                        stt(bnd16[:, 1, v, 1:], pf[:, 0, 1:], clip, bnd16[:, 0, v, 1:], ALU.mult,
                            ALU.subtract).then_inc(sem["bound_all"], 1)
                if point == LAST["mb", 0] and exists(k, 1):
                    dve.wait_ge(sem["mb_ready"], j + 1)
                    b = bank("mb")
                    since(dve, "tt_done", 2 * j)
                    tt(mT[:, q], b[:, 0:P], tri, ALU.mult)
                    tsc(nbh[:], b[:, P:P + NS], -1.0, None, ALU.mult).then_inc(sem["nb16"], 1)
                    dve.wait_ge(sem["nb16"], 2 * j + 1)
                    stt(nbl[:], b[:, P:P + NS], -1.0, nbh[:], ALU.mult, ALU.subtract).then_inc(sem["nb16"], 1)
                    dve.wait_ge(sem["nb16"], 2 * j + 2)
                    since(dve, "carry_ready", 2 * j)
                    for h, src in enumerate((nbh, nbl)):
                        for d in range(2):
                            last = tt(bqm[:, h, :, d],
                                      src[:].rearrange("s (o n) -> s o n", o=1).broadcast_to([P, NSUB, NS]),
                                      prefix.rearrange("s (j o) -> s j o", o=1).broadcast_to([P, NSUB, NS]),
                                      ALU.mult)
                    last.then_inc(sem["mb_taken"], 1)
                for i in range(2):
                    tap, odd = divmod(point - CONV_AT[i] + 1, 2)
                    if not odd and 1 <= tap < TAPS and exists(k, 2):
                        n = 2 * (k + 2) + i
                        dve.wait_ge(sem["tap0"], n + 1)
                        since(dve, "tap", (TAPS - 1) * n + tap - 1)
                        for d in range(4 * i, 4 * i + 4):
                            last = stt(conv[:, d, :], xr[:, p, d, tap:tap + P], cols[:, d, 3 + tap:4 + tap],
                                       conv[:, d, :], ALU.mult, ALU.add)
                        last.then_inc(sem["tap"], 1)
                    if odd and tap == TAPS - 1 and exists(k, 2):
                        dve.wait_ge(sem["tap"], (TAPS - 1) * (2 * (k + 2) + i + 1))
                        nc.vector.tensor_copy(xr[:, p, 4 * i:4 * i + 4, 0:TAPS - 1],
                                              xr[:, p, 4 * i:4 * i + 4, P:P + TAPS - 1]).then_inc(sem["conv_done"], 1)
                for i in range(2):
                    if point != LAST["hend", i] or not exists(k, -1):
                        continue
                    half = slice(i * BANK, (i + 1) * BANK)
                    dve.wait_ge(sem["hend_ready"], 2 * (k - 1) + i + 1)
                    dve.wait_ge(sem["carry_taken"], 2 * k)
                    if exists(k, 0):
                        dve.wait_ge(sem["h1_high"], k + 1)
                        dve.wait_ge(sem["h1_low"], k + 1)
                    stt(h1[:, half], lend[:, (k - 1) % 2 if isinstance(k, int) else (p + 1) % 2, half], -1.0,
                        bank("hend", i)[0:NS], ALU.mult, ALU.add).then_inc(sem["hend_taken"], 1)
                if point == 35 and exists(k, 1):
                    dve.wait_ge(sem["row_in"], 16 * (j + 1))
                    if first_chunk(j):
                        since(dve, "h1_high", j)
                        since(dve, "h1_low", j)
                        tsc(h1[:], xn0, zT[:, 0, 0:1], None, ALU.mult).then_inc(sem["h1_raw"], 1)
                    else:
                        dve.wait_ge(sem["h_scaled"], k)
                        stt(h1[:], xn0, zT[:, 0, 0:1], h1[:], ALU.mult, ALU.add).then_inc(sem["h1_raw"], 1)
                    dve.wait_ge(sem["h1_raw"], j + 1)
                    tsc(h1[:], h1[:], CLIP, -CLIP, ALU.min, ALU.max).then_inc(sem["h1_done"], 1)
                for i in range(2):
                    if point != LAST["carry", i] + 1 or not exists(k, 1):
                        continue
                    half = slice(i * BANK, (i + 1) * BANK)
                    dve.wait_ge(sem["carry16"], 2 * j + i + 1)
                    dve.wait_ge(sem[f"xstack_in{q}"], N_XSTACK * pair(k, p, 1))
                    since(dve, "hend_taken", 2 * k)
                    nc.vector.tensor_copy(lend[:, q, half], bank("carry", i)[0:NS])
                    stt(cc[:, half], ch[:, half], neg_low, bank("carry", i), ALU.mult, ALU.add
                        ).then_inc(sem["carry_taken"], 1)
                if point == LAST["cr", 0] and exists(k, 0):
                    dve.wait_ge(sem["cr_ready"], k + 1)
                    since(dve, "y_ready", DB * k)
                    rep = bank("cr")[:, 0:P].rearrange("r (g e i) -> r g e i", g=4, e=4)
                    d = delta.rearrange("r (o i) -> r o i", o=1).broadcast_to([P, 4, WAYS])
                    for e in range(4):
                        last = tt(cst[:, :, e, WAYS * e:WAYS * (e + 1)], rep[:, :, e], d, ALU.mult)
                    last.then_inc(sem["cr_taken"], 1)
                for i in range(2):
                    if point != LAST["yT", i] + 1 or not exists(k, -1):
                        continue
                    dve.wait_ge(sem["yT_high"], 2 * (k - 1) + i + 1)
                    stt(yT[:, 1, 4 * i:4 * i + 4, :], bank("yT", i).rearrange("d (e t) -> d e t", e=4), 1.0,
                        yT[:, 0, 4 * i:4 * i + 4, :], ALU.mult, ALU.subtract).then_inc(sem["yT_taken"], 1)
                if point == LAST["out", 0] and exists(k, -1):
                    dve.wait_ge(sem["out_ready"], k)
                    dve.wait_ge(sem["res_in"], 16 * k)
                    stt(res[:], bank("out"), 1 / WS, res[:], ALU.mult, ALU.add).then_inc(sem["out_taken"], 1)

            def y_copy(k, p, u):
                dve.wait_ge(sem["y_ready"], DB * k + u + 1)
                if u % 4 == 0:
                    since(dve, "yT_ready", 2 * (k - 1) + u // 4 + 1)
                cut = slice(u * P, (u + 1) * P)
                nc.vector.tensor_copy(y[:, cut], bank("y", u)[:, 0:P]).then_inc(sem["y_taken"], 1)

            def ends(k, p, u):
                dve.wait_ge(sem["scanned"], TILES * k + NQ * (u + 1))
                since(dve, "hend_ready", 2 * (k - 1))
                nc.vector.tensor_copy(kend[:, p, u, :], ks[:, u % 2, :, P - 1]).then_inc(sem["kend_done"], 1)

            def body(k, p):
                def scan(s):
                    u, q = divmod(s, NQ)
                    g = TILES * k + s
                    dve.wait_ge(sem["lower_ready"], g + 1)
                    dve.wait_ge(sem["upper_copied"], g + 1)
                    if q == 0:
                        since(dve, "flipped", TILES * k + NQ * (u - 1))
                        since(dve, "kend_done", DB * k + u - 1)
                    nc.vector.tensor_tensor_scan(ks[:, u % 2, QN * q:QN * (q + 1)].rearrange("d n t -> d (n t)"),
                                                 ps_low[:, s % 2], upper[:, s % RING], 0.0,
                                                 ALU.max, ALU.min).then_inc(sem["scanned"], 1)

                for s in range(TILES):
                    if exists(k, 0) and s == 0:
                        scan(0)
                    late = (s + 1) % NQ == 0
                    if exists(k, 0) and s + 1 < TILES and not late:
                        scan(s + 1)
                    if s == 0 and exists(k, -1):
                        ends(k - 1, 1 - p, DB - 1)
                    if s % NQ == 0 and s and exists(k, 0):
                        ends(k, p, s // NQ - 1)
                    for point in (2 * s, 2 * s + 1):
                        if point % 2 and exists(k, 0) and s + 1 < TILES and late:
                            scan(s + 1)
                        for _, _, name, i, off, _ in JOBS:
                            if name == "y" and LAST["y", i] == point and exists(k, off):
                                y_copy(k + off, (p + off) % 2, i)
                        side(k, p, point)

            steps(dve, body)

        @block.gpsimd
        def _(pool):
            tt, tsc = nc.gpsimd.tensor_tensor, nc.gpsimd.tensor_scalar
            pool.wait_ge(sem["const_in"], N_CONST)
            pool.wait_ge(sem["prep"], 1)
            pool.wait_ge(sem["fixed_in"], N_FIXED)

            def body(k, p):
                j, q = k + 1, (p + 1) % 2
                for s in range(TILES):
                    if s == 1 and exists(k, 1):
                        pool.wait_ge(sem["norm_in"], j + 1)
                        since(pool, "z1", j)
                        tt(tiny[:, 1:2], tiny[:, 0:1], halfs[:, 0:1], ALU.pow).then_inc(sem["rstd"], 1)
                    if s == 7 and exists(k, 1):
                        pool.wait_ge(sem["xa"], j + 1)
                        tt(xn[:, q], xn[:, q], row_g[:], ALU.mult).then_inc(sem["xg"], 1)
                        pool.wait_ge(sem["xg"], j + 1)
                        tt(xn[:, q], xn[:, q], row_b[:], ALU.add).then_inc(sem["xn_done"], 1)
                    if s == 6 and exists(k, -1):
                        gated(k - 1, 1 - p, 1)
                    if s == 10 and exists(k, 1):
                        pool.wait_ge(sem["squares"], j + 1)
                        tt(tiny[:, 5:6], tiny[:, 4:5], halfs[:, 1:2], ALU.pow).then_inc(sem["root"], 1)
                        pool.wait_ge(sem["root"], j + 1)
                        carrier(p)
                        tsc(tiny[:, 6:7], tiny[:, 5:6], 1.0, 0.0, ALU.min, ALU.max).then_inc(sem["nrm"], 1)
                        pool.wait_ge(sem["xh_done"], j + 1)
                        since(pool, f"stack_in{1 - q}", N_STACK * pair(k, p, 0))
                        tt(xl[:], xn[:, q], xh[:], ALU.subtract).then_inc(sem["xl_done"], 1)
                    if s == 13 and exists(k, 2):
                        pool.wait_ge(sem["xT_high"], k + 3)
                        tt(x16[:, 1], xf[:], x16[:, 0], ALU.subtract).then_inc(sem["xT_low"], 1)
                    if s == 27 and exists(k, 1):
                        pool.wait_ge(sem["xs_high"], k + 2)
                        tt(x16[:, 1], xf[:], x16[:, 0], ALU.subtract).then_inc(sem["xs_low"], 1)
                    if s in (6, 23) and exists(k, 0):
                        i = s // 23
                        half = slice(i * BANK, (i + 1) * BANK)
                        since(pool, "y_ready", DB * k + 4 * i)
                        tt(dx[:], xn[:, p, half], row_d[:, half], ALU.mult).then_inc(sem["dx_done"], 1)
                    if s == 21 and exists(k, 1):
                        pool.wait_ge(sem["nb16"], 2 * (j + 1))
                        since(pool, f"stack_in{1 - q}", N_STACK * pair(k, p, 0))
                        m = submask.rearrange("s (o t) -> s o t", o=1).broadcast_to([P, NS, SUB])
                        for src, dst in ((nbh, tth), (nbl, ttl)):
                            tt(dst[:], src[:].rearrange("s (n o) -> s n o", o=1).broadcast_to([P, NS, SUB]), m,
                               ALU.mult).then_inc(sem["tt_done"], 1)
                    if s == 19 and exists(k, 1):
                        pool.wait_ge(sem["h1_high"], j + 1)
                        tt(h16[:, 1], h1[:], h16[:, 0], ALU.subtract).then_inc(sem["h1_low"], 1)
                    if s == 24 and exists(k, 0):
                        gated(k, p, 0)

            def carrier(p):
                tt(idle[:, p:p + 1], halfs[:, 0:1], halfs[:, 1:2], ALU.mult)

            def gated(k, p, i):
                pool.wait_ge(sem["y_taken"], DB * k + 4 * (i + 1))
                pool.wait_ge(sem["gate_taken"], 2 * k + i + 1)
                half = slice(i * BANK, (i + 1) * BANK)
                tt(y[:, half], y[:, half], gate[:, half], ALU.mult).then_inc(sem["y_gated"], 1)

            steps(pool, body)


_OUT = "out_dram"


def kernel(x, cond_2048, L0_cond_W_in, L0_cond_W_conv, L0_cond_b_conv, L0_cond_ln_g, L0_cond_ln_b,
           L0_cond_W_xproj, L0_cond_W_dt, L0_cond_b_dt, L0_cond_A_log, L0_cond_D, L0_cond_W_out):
    import concourse.bacc as bacc
    from concourse.bass_utils import run_bass_kernel_spmd

    def col(v):
        return np.asarray(v).reshape(DB, P).T[:, :, None]

    taps = np.asarray(L0_cond_W_conv).reshape(DB, P, TAPS).transpose(1, 0, 2)
    cond = np.asarray(cond_2048).reshape(BATCH, DB, P).transpose(2, 1, 0)
    arrays = {
        "x": np.asarray(x).reshape(BATCH, SEQ // P, P, DM)[:, :, row_steps()].reshape(BATCH, SEQ, DM),
        "xT": np.asarray(x).transpose(0, 2, 1),
        "xTs": np.asarray(x).reshape(BATCH, SEQ // P, P, DM)[:, :, row_steps()].reshape(BATCH, SEQ, DM
                                                                                   ).transpose(0, 2, 1),
        "w_inT": np.asarray(L0_cond_W_in).T,
        "w_outT": np.asarray(L0_cond_W_out).T,
        "wxT": np.asarray(L0_cond_W_xproj).T,
        "cols": np.concatenate([col(L0_cond_ln_g), col(L0_cond_ln_b), col(L0_cond_b_conv), taps, cond], axis=2),
        "small": np.concatenate([np.asarray(L0_cond_W_dt).T, np.zeros((NS, 2 * NS), np.float32),
                                 np.asarray(L0_cond_b_dt)[:, None],
                                 np.asarray(L0_cond_A_log)[:, None]], axis=1),
        "rows": np.stack([np.asarray(v) for v in (L0_cond_ln_g, L0_cond_ln_b, L0_cond_D)]),
        **shape_constants(),
    }
    nc = bacc.Bacc("TRN2", target_bir_lowering=False, num_devices=1)
    ins, aps = {}, {}
    for name, a in arrays.items():
        a = np.ascontiguousarray(a)
        ins[f"in_{name}"] = a
        aps[name] = nc.dram_tensor(f"in_{name}", a.shape, mybir.dt.from_np(a.dtype), kind="ExternalInput").ap()
    out = nc.dram_tensor(_OUT, (BATCH, SEQ, DM), mybir.dt.float32, kind="ExternalOutput").ap()
    scratch = nc.dram_tensor("bounds_dram", (2, NSUB, 2, NS, SUB), mybir.dt.float16, kind="Internal").ap()
    row = nc.dram_tensor("row_dram", (1, DI), mybir.dt.float32, kind="Internal").ap()
    build(nc, aps, out, scratch, row)
    r = run_bass_kernel_spmd(nc, [ins], core_ids=[0])
    rows = np.asarray(r.results[0][_OUT]).reshape(BATCH, SEQ // P, P, DM)
    return rows[:, :, np.argsort(row_steps())].reshape(BATCH, SEQ, DM)
```
